# Optimizing a Trainium2 kernel written in Bass

```python
import numpy as np
import jax
import jax.numpy as jnp

def _softmax(x, axis=-1):
    return jax.nn.softmax(x, axis=axis)

def _gelu(x):
    return jax.nn.gelu(x, approximate=True)

def _silu(x):
    return jax.nn.silu(x)

def _sigmoid(x):
    return jax.nn.sigmoid(x)

def _layernorm(x, axis=-1, eps=1e-05):
    m = jnp.mean(x, axis=axis, keepdims=True)
    v = jnp.var(x, axis=axis, keepdims=True)
    return (x - m) / jnp.sqrt(v + eps)

def _scatter_add(tgt, idx, src, axis=0):
    return tgt.at[idx].add(src)

def _segment_sum(src, seg, n):
    return jax.ops.segment_sum(src, seg, n)
kernel_name = 'mk_gnn_resnorm_d1_gnn_r8_215ba6'

def setup_inputs(seed: int=0):
    np.random.seed(seed)
    _w = jnp.asarray

    def _rec_inputs():
        import jax
        import jax.numpy as jnp
        _gk = jax.random.key(seed)
        x = -0.0003713 + 1 * jax.random.normal(jax.random.fold_in(_gk, 1), (12500, 128), jnp.float32)
        _s = jax.random.randint(jax.random.fold_in(_gk, 2), (100000,), 0, 12500, jnp.int32)
        _d = jax.random.randint(jax.random.fold_in(_gk, 3), (100000,), 0, 12500, jnp.int32)
        _loop = jnp.arange(12500, dtype=jnp.int32)
        src = jnp.concatenate([_s, _d, _loop])
        dst = jnp.concatenate([_d, _s, _loop])
        _o = jnp.argsort(dst, stable=True)
        src = src[_o]
        dst = dst[_o]
        return (x, src, dst)
    x, src, dst = _rec_inputs()

    def _L0_gnn_setup():
        import jax, jax.numpy as jnp
        import numpy as np
        N_VAR, N_FAC, N_EDGE, D = (12500, 6250, 125000, 128)
        key = jax.random.key(seed)
        ks = jax.random.split(key, 8)
        return {'variables': jax.random.normal(ks[0], (N_VAR, D), dtype=jnp.float32), 'factors': jax.random.normal(ks[1], (N_FAC, D), dtype=jnp.float32), 'senders': jax.random.randint(ks[2], (N_EDGE,), 0, N_VAR), 'receivers': jax.random.randint(ks[3], (N_EDGE,), 0, N_FAC), 'Wm': jax.random.normal(ks[4], (2 * D, D), dtype=jnp.float32) * (1.0 / np.sqrt(2 * D)), 'bm': jnp.zeros((D,), dtype=jnp.float32), 'Wc': jax.random.normal(ks[5], (2 * D, D), dtype=jnp.float32) * (1.0 / np.sqrt(2 * D)), 'bc': jnp.zeros((D,), dtype=jnp.float32)}
    _L0_gnn_all = _L0_gnn_setup()
    _L0_gnn_in = {k: v for k, v in _L0_gnn_all.items() if k in ('factors', 'Wm', 'bm', 'Wc', 'bc')}
    del _L0_gnn_all
    return {'x': x, 'src': src, 'dst': dst, 'L0_gnn_factors': _L0_gnn_in['factors'], 'L0_gnn_Wm': _L0_gnn_in['Wm'], 'L0_gnn_bm': _L0_gnn_in['bm'], 'L0_gnn_Wc': _L0_gnn_in['Wc'], 'L0_gnn_bc': _L0_gnn_in['bc']}

def reference(x, src, dst, L0_gnn_factors, L0_gnn_Wm, L0_gnn_bm, L0_gnn_Wc, L0_gnn_bc):
    import jax
    import jax.numpy as jnp

    def _L0_gnn_ref(variables, factors, senders, receivers, Wm, bm, Wc, bc):
        import jax, jax.numpy as jnp
        import numpy as np
        N_VAR, N_FAC, N_EDGE, D = (12500, 6250, 125000, 128)
        x_i = variables[senders]
        x_j = factors[receivers]
        x = jnp.concatenate([x_i, x_j], axis=-1)
        msg = jax.nn.relu(x @ Wm + bm)
        agg = jax.ops.segment_sum(msg, senders, num_segments=variables.shape[0])
        h = jnp.concatenate([variables, agg], axis=-1)
        h = jax.nn.relu(h @ Wc + bc)
        return variables + h
    x = _layernorm(x + _L0_gnn_ref(x, L0_gnn_factors, src, dst, L0_gnn_Wm, L0_gnn_bm, L0_gnn_Wc, L0_gnn_bc), axis=-1)
    return x

_drawn_inputs = setup_inputs


def setup_inputs(seed=0):
    import zlib

    import numpy as np

    out = dict(_drawn_inputs(seed))
    spreads = {'L0_gnn_bm': (0.0, 0.1), 'L0_gnn_bc': (0.0, 0.518)}
    factors = {}
    for name, (base, spread) in spreads.items():
        noise = np.random.default_rng([zlib.crc32(name.encode()), seed]).standard_normal(out[name].shape)
        drawn = base * np.exp(spread * noise) if base else spread * noise
        out[name] = jnp.asarray(drawn.astype(out[name].dtype))
    for name, factor in factors.items():
        out[name] = (out[name] * factor).astype(out[name].dtype)
    return out
```

```python
from contextlib import ExitStack

import concourse.bass as bass
from concourse import mybir

ALU = mybir.AluOpType
ACT = mybir.ActivationFunctionType
F32 = mybir.dt.float32
BF16 = mybir.dt.bfloat16
I32 = mybir.dt.int32
AX_X = mybir.AxisListType.X

P = 128
G = 4
BIG = float(1 << 20)
BLANK = 128
BANK = 512
SLAB = 7


def gnn_kernel(nc, x, src, dst, factors, Wm, bm, Wc, bc, out):
    N, D = x.shape
    F = factors.shape[0]
    E = src.shape[0]
    LAST = F - 1
    NB = -(-N // P)
    FB = -(-F // P)
    NTAIL, FTAIL = N - (NB - 1) * P, F - (FB - 1) * P
    CH = -(-E // (P * P))
    NT = CH * P
    HALF = 16
    BODY = 2 * HALF
    NFLAG = NT // HALF
    full_rows = (E - (CH - 1) * P * P) // P
    rest = E - (CH - 1) * P * P - full_rows * P
    SBODY = 4 * G
    ST = -(-(-(-E // P) + NB) // SBODY) * SBODY
    SCH = -(-(ST + SBODY) // P)
    STP = SCH * P
    GW = G * NB
    assert D == P and GW <= BANK and NT % BODY == 0 and NB % SLAB == 0 and FB % SLAB == 0
    assert (NB // SLAB) % 2 == 0 and (FB // SLAB) % 2 == 1 and STP * P < BIG
    FQ = FB // SLAB
    XQ = NB // SLAB
    RING = 4
    CBODY = 16
    GROUPS = NT // G
    TURNS = -(-CH // 4)
    STURNS = -(-SCH // 4)
    assert RING * G == HALF and GROUPS % (2 * CBODY) == 0 and GROUPS // CBODY >= FQ + XQ and STP * 7 == NB * D

    sorted_list = nc.dram_tensor("sorted_list", (STP * P, 1), F32).ap()
    B_rows = nc.dram_tensor("B_rows", (FB * P, D), F32).ap()

    with ExitStack() as ctx:
        def sb(name, shape, dt=F32):
            return ctx.enter_context(nc.sbuf_tensor(name, shape, dt))

        def sem(name):
            return ctx.enter_context(nc.semaphore(name))

        bank = [ctx.enter_context(nc.psum_tensor(f"bank{i}", [P, BANK], F32)) for i in range(8)]
        ranks_ps, counts_ps, clamped_ps = bank[0], bank[1], bank[2]

        ident = sb("ident", [P, P])
        iota_lo = sb("iota_lo", [P, P])
        iota_clamped = sb("iota_clamped", [P, P], BF16)
        iota_hi = sb("iota_hi", [P, NB], BF16)
        before = sb("before", [P, P], BF16)
        from_on = sb("from_on", [P, P], BF16)
        ones_bf = sb("ones_bf", [P, P], BF16)
        ones_f = sb("ones_f", [P, P])
        zeros_bf = sb("zeros_bf", [P, GW], BF16)
        eps = sb("eps", [P, 1])
        wm = sb("wm", [P, 2, D])
        wc = sb("wc", [P, 2, D])
        bm_row = sb("bm_row", [1, D])
        bc_row = sb("bc_row", [1, D])
        b_last = sb("b_last", [P, D])

        hi_n = sb("hi_n", [P, NT])
        hi_all = sb("hi_all", [P, NT])
        lo_c = sb("lo_c", [P, NT])
        value = sb("value", [P, NT])
        place = sb("place", [P, NT])
        edge_raw = sb("edge_raw", [P, 2, STP], I32)
        edge_row = sb("edge_row", [P, 3, NT])
        A = sb("A", [P, NB, D])
        agg = sb("agg", [P, NB, D])

        oh_n = sb("oh_n", [P, 4, G, NB], BF16)
        oh_lo = sb("oh_lo", [P, 2, G, P], BF16)
        oh_hi = sb("oh_hi", [P, 2, G, NB], BF16)
        count = sb("count", [P, G, NB])
        start_at = sb("start_at", [P, G, NB])
        small = sb("small", [P, 6, NB])
        small_i = sb("small_i", [P, 2, NB], I32)
        tile_end = sb("tile_end", [P, 2])
        flag = sb("flag", [1, NFLAG], I32)
        flag_f = sb("flag_f", [1, NFLAG])
        landed_f = sb("landed_f", [1, NFLAG + 2])
        landed = sb("landed", [1, NFLAG + 2], I32)
        bodies = sb("bodies", [1, 1], I32)
        addr_now = sb("addr_now", [P, 2, HALF], I32)
        rank_now = sb("rank_now", [P, RING * G])
        value_now = sb("value_now", [P, 2, HALF])

        dst_now = sb("dst_now", [P, 4, G], I32)
        clamped_count = sb("clamped_count", [P, NB])
        stage = sb("stage", [P, 4 * SLAB * D])
        slabT = sb("slabT", [P, 2, SLAB * D])
        stats = sb("stats", [P, SLAB, 6])
        mv = sb("mv", [P, SLAB, 2])
        rstd = sb("rstd", [P, 2, SLAB])


        A_flat = A[:].rearrange("p a b -> p (a b)")
        agg_flat = agg[:].rearrange("p a b -> p (a b)")
        blank_fill = agg_flat[:, 0:STP]
        block_le = agg_flat[:, STP:2 * STP]
        tile_iota = agg_flat[:, 2 * STP:3 * STP]
        is_sorted = agg_flat[:, 3 * STP:3 * STP + NT]
        row_flat = edge_row[:].rearrange("p a b -> p (a b)")
        raw_flat = edge_raw[:].rearrange("p a b -> p (a b)")
        sorted_rows = row_flat[:, 0:STP]
        dst_s = row_flat[:, STP:2 * STP]
        lo_s = raw_flat[:, 0:STP].bitcast(F32)
        block_of = raw_flat[0:1, STP:2 * STP]
        raw_i = hi_n[:].bitcast(I32)
        sort_i = hi_n[:, 0:BANK].bitcast(I32)
        sort_d = hi_n[:, BANK:2 * BANK].bitcast(I32)
        sort_l = hi_n[:, 2 * BANK:3 * BANK].bitcast(I32)
        oh_s = hi_all[:, 0:2 * G * P].rearrange("p (s m) -> p s m", s=2)
        oh_sT = lo_c[:, 0:2 * G * P].rearrange("p (s m) -> p s m", s=2)
        pre = value[:, 0:2 * G * D].rearrange("p (s m) -> p s m", s=2)
        msg = place[:, 0:2 * G * D].rearrange("p (s m) -> p s m", s=2)
        slab = stage[:, 0:2 * SLAB * D].rearrange("p (s m) -> p s m", s=2)
        outs = stage[:, 2 * SLAB * D:4 * SLAB * D].rearrange("p (s m) -> p s m", s=2)
        B_now = stage[:, 0:4 * G * D].rearrange("p (s k d) -> p s k d", s=4, k=G)
        aggT = A_flat[:, 0:SLAB * D]
        resid = A_flat[:, SLAB * D:2 * SLAB * D]
        agg_now = A_flat[:, 2 * SLAB * D:4 * SLAB * D].rearrange("p (s m) -> p s m", s=2)
        fac_tiles = factors[0:(FB - 1) * P].rearrange("(t p) d -> p t d", p=P)
        x_tiles = x[0:(NB - 1) * P].rearrange("(t p) d -> p t d", p=P)
        out_tiles = out[0:(NB - 1) * P].rearrange("(t p) d -> p t d", p=P)
        B_tiles = B_rows.rearrange("(t p) d -> p t d", p=P)
        halves = [(c, min(BANK, SLAB * D - c)) for c in range(0, SLAB * D, BANK)]

        s_blank_edges = sem("s_blank_edges")
        s_edges = sem("s_edges")
        s_weights = sem("s_weights")
        s_slab_blank = sem("s_slab_blank")
        s_slab = [sem(f"s_slab{k}") for k in range(2)]
        s_blank_fill = sem("s_blank_fill")
        s_slab_out = sem("s_slab_out")
        s_B_stored = [sem(f"s_B_stored{k}") for k in range(2)]
        s_b_last = sem("s_b_last")
        s_slab_T = sem("s_slab_T")
        s_sorted = sem("s_sorted")
        s_list_back = sem("s_list_back")
        s_sums_done = sem("s_sums_done")
        s_x = [sem(f"s_x{k}") for k in range(2)]
        s_y = sem("s_y")
        s_out = [sem(f"s_out{k}") for k in range(2)]
        s_ones = sem("s_ones")
        s_const = sem("s_const")
        s_offsets = sem("s_offsets")
        s_staged = sem("s_staged")
        s_scatter = [sem(f"s_scatter{k}") for k in range(2)]
        s_receivers = sem("s_receivers")
        s_gather = [sem(f"s_gather{k}") for k in range(4)]
        s_slab_copied = sem("s_slab_copied")
        s_slab_mm = sem("s_slab_mm")
        s_ranked = sem("s_ranked")
        s_placed = sem("s_placed")
        s_sort_cols = sem("s_sort_cols")
        s_oh_turned = sem("s_oh_turned")
        s_oh_copied = sem("s_oh_copied")
        s_added = sem("s_added")
        s_sum_free = sem("s_sum_free")
        s_msg = sem("s_msg")
        s_x_turned = sem("s_x_turned")
        s_xT = sem("s_xT")
        s_h = sem("s_h")
        s_resid = sem("s_resid")
        s_relu = sem("s_relu")
        s_var = sem("s_var")
        s_std = sem("s_std")
        s_step = sem("s_step")
        s_rows = sem("s_rows")
        s_turned = sem("s_turned")
        s_cols = sem("s_cols")
        s_count_free = sem("s_count_free")
        s_count_oh = sem("s_count_oh")
        s_flags = sem("s_flags")
        s_ends = sem("s_ends")
        s_block_le = sem("s_block_le")
        s_blocks = sem("s_blocks")
        s_block_of = sem("s_block_of")
        s_rank_free = sem("s_rank_free")
        s_rank_oh = sem("s_rank_oh")
        s_hist_free = sem("s_hist_free")
        s_hist_oh = sem("s_hist_oh")
        s_before = sem("s_before")
        s_clamped_add = sem("s_clamped_add")
        s_sort_turned = sem("s_sort_turned")
        s_oh_s = sem("s_oh_s")
        s_spread = sem("s_spread")
        s_agg = sem("s_agg")
        s_agg_free = sem("s_agg_free")
        s_agg_now = sem("s_agg_now")
        s_aT = sem("s_aT")
        s_stats = sem("s_stats")
        s_recip = sem("s_recip")
        s_zeroed = sem("s_zeroed")
        block = ctx.enter_context(nc.Block())

        def by_tile(slab_ap):
            return slab_ap.rearrange("p (t d) -> p t d", d=D)

        def load_slab(eng, dest, tiles, whole, a, tail, semaphore, last):
            dest = by_tile(dest)
            if not last:
                eng.dma_start(dest, tiles[:, bass.ds(a * SLAB, SLAB), :]).then_inc(semaphore, 32)
                return
            first = a * SLAB
            eng.dma_start(dest[:, 0:SLAB - 1, :], tiles[:, first:first + SLAB - 1, :]).then_inc(semaphore, 16)
            eng.dma_start(dest[0:tail, SLAB - 1, :], whole[(first + SLAB - 1) * P:, :]).then_inc(semaphore, 16)

        @block.sync
        def _(sp):
            sp.wait_ge(s_blank_edges, 1)
            for k, edges in enumerate((src, dst)):
                whole = edges[0:(CH - 1) * P * P].rearrange("(c r e) -> r c e", r=P, e=P)
                sp.dma_start(edge_raw[:, k, 0:(CH - 1) * P].rearrange("r (c e) -> r c e", e=P), whole)\
                    .then_inc(s_edges, 16)
                part = edges[(CH - 1) * P * P:E - rest].rearrange("(r e) -> r e", e=P)
                sp.dma_start(edge_raw[0:full_rows, k, (CH - 1) * P:NT], part).then_inc(s_edges, 16)
                if rest:
                    sp.dma_start(edge_raw[full_rows:full_rows + 1, k, (CH - 1) * P:(CH - 1) * P + rest],
                                 edges[E - rest:E].rearrange("(a e) -> a e", a=1)).then_inc(s_edges, 16)
            sp.dma_start(wm[:], Wm.rearrange("(k p) n -> p k n", p=P)).then_inc(s_weights, 16)
            sp.dma_start(wc[:], Wc.rearrange("(k p) n -> p k n", p=P)).then_inc(s_weights, 16)
            sp.dma_start(bm_row[:], bm.rearrange("(a d) -> a d", a=1)).then_inc(s_weights, 16)
            sp.dma_start(bc_row[:], bc.rearrange("(a d) -> a d", a=1)).then_inc(s_weights, 16)
            sp.wait_ge(s_slab_blank, 1)
            load_slab(sp, slab[:, 0], fac_tiles, factors, 0, FTAIL, s_slab[0], False)
            load_slab(sp, slab[:, 1], fac_tiles, factors, 1, FTAIL, s_slab[1], False)

            for q in range(FQ):
                sp.wait_ge(s_slab_out, q + 2)
                sp.dma_start(B_tiles[:, q * SLAB:(q + 1) * SLAB, :], by_tile(outs[:, q % 2]))\
                    .then_inc(s_B_stored[q % 2], 16)
                n = q + 2
                if n < FQ:
                    load_slab(sp, slab[:, n % 2], fac_tiles, factors, n, FTAIL, s_slab[n % 2], n == FQ - 1)
                else:
                    load_slab(sp, slab[:, n % 2], x_tiles, x, n - FQ, NTAIL, s_slab[n % 2], False)
            sp.wait_ge(s_B_stored[0], 16 * ((FQ + 1) // 2))
            sp.wait_ge(s_B_stored[1], 16 * (FQ // 2))
            sp.dma_start(b_last[:], B_rows[LAST:LAST + 1, :].to_broadcast([P, D])).then_inc(s_b_last, 16)
            with sp.Fori(0, (XQ - 4) // 2) as i:
                for k in range(2):
                    sp.wait_ge(s_slab_T, i * 2 + (FQ + k + 1))
                    load_slab(sp, slab[:, (FQ + k) % 2], x_tiles, x, i * 2 + (2 + k), NTAIL,
                              s_slab[(FQ + k) % 2], False)
            for a in (XQ - 2, XQ - 1):
                sp.wait_ge(s_slab_T, FQ + a - 1)
                load_slab(sp, slab[:, (FQ + a) % 2], x_tiles, x, a, NTAIL, s_slab[(FQ + a) % 2], a == XQ - 1)

            sp.wait_ge(s_sorted, 1)
            sp.dma_start(sorted_rows.rearrange("r (c e) -> r c e", e=P),
                         sorted_list.rearrange("(c r e) a -> r c (e a)", r=P, e=P)).then_inc(s_list_back, 16)

            sp.wait_ge(s_sums_done, 1)
            load_slab(sp, slab[:, 0], x_tiles, x, 0, NTAIL, s_x[0], False)
            load_slab(sp, slab[:, 1], x_tiles, x, 1, NTAIL, s_x[1], False)

            def store_out(a, slot, last):
                sp.wait_ge(s_y, a + 1)
                rows = by_tile(outs[:, slot])
                if not last:
                    sp.dma_start(out_tiles[:, bass.ds(a * SLAB, SLAB), :], rows).then_inc(s_out[slot], 32)
                else:
                    sp.dma_start(out_tiles[:, a * SLAB:a * SLAB + SLAB - 1, :], rows[:, 0:SLAB - 1, :])\
                        .then_inc(s_out[slot], 16)
                    sp.dma_start(out[(NB - 1) * P:N, :], rows[0:NTAIL, SLAB - 1, :]).then_inc(s_out[slot], 16)

            with sp.Fori(0, (XQ - 4) // 2) as i:
                for k in range(2):
                    store_out(i * 2 + k, k, False)
                    load_slab(sp, slab[:, k], x_tiles, x, i * 2 + (2 + k), NTAIL, s_x[k], False)
            for a in range(XQ - 4, XQ):
                store_out(a, a % 2, a == XQ - 1)
                if a + 2 < XQ:
                    load_slab(sp, slab[:, a % 2], x_tiles, x, a + 2, NTAIL, s_x[a % 2], a + 2 == XQ - 1)
            for k in range(2):
                sp.wait_ge(s_out[k], 32 * (XQ // 2))

        @block.gpsimd
        def _(pool):
            pool.memset(edge_raw[:, :, (CH - 1) * P:NT], 32767).then_inc(s_blank_edges, 1)
            pool.memset(stage[:], 0.0).then_inc(s_slab_blank, 1)
            pool.memset(ones_f[:], 1.0).then_inc(s_ones, 1)
            pool.memset(ones_bf[:], 1.0).then_inc(s_ones, 1)
            pool.wait_ge(s_ones, 2)
            pool.affine_select(out=ident[:], in_=ones_f[:], compare_op=ALU.is_equal, fill=0.0, base=0,
                               pattern=[[1, P]], channel_multiplier=-1).then_inc(s_const, 1)
            pool.iota(iota_hi[:], [[1, NB]], base=0, channel_multiplier=0,
                      allow_small_or_imprecise_dtypes=True).then_inc(s_const, 1)
            pool.memset(zeros_bf[:], 0.0).then_inc(s_const, 1)
            pool.iota(iota_clamped[:], [[1, P]], base=0, channel_multiplier=0,
                      allow_small_or_imprecise_dtypes=True).then_inc(s_const, 1)
            pool.iota(iota_lo[:], [[1, P]], base=0, channel_multiplier=0,
                      allow_small_or_imprecise_dtypes=True).then_inc(s_const, 1)
            pool.affine_select(out=before[:], in_=ones_bf[:], compare_op=ALU.is_gt, fill=0.0, base=0,
                               pattern=[[1, P]], channel_multiplier=-1).then_inc(s_const, 1)
            pool.affine_select(out=from_on[:], in_=ones_bf[:], compare_op=ALU.is_ge, fill=0.0, base=0,
                               pattern=[[-1, P]], channel_multiplier=1).then_inc(s_const, 1)
            pool.memset(eps[:], 1e-5).then_inc(s_const, 1)
            pool.memset(blank_fill, float(BLANK)).then_inc(s_blank_fill, 1)
            pool.iota(tile_iota, [[1, STP]], base=0, channel_multiplier=0,
                      allow_small_or_imprecise_dtypes=True).then_inc(s_const, 1)

            pool.wait_ge(s_blank_fill, 1)
            for h in range(2):
                rows = slice(h * (STP * P // 2), (h + 1) * (STP * P // 2))
                pool.dma_start(sorted_list[rows].rearrange("(p n) a -> p (n a)", p=P), blank_fill[:, 0:STP // 2])\
                    .then_inc(s_scatter[h], 16)
            for h in range(2):
                pool.wait_ge(s_scatter[h], 16)
            pool.wait_ge(s_offsets, 1)
            with pool.Fori(0, NT // BODY) as i:
                for h in range(2):
                    pool.wait_ge(s_staged, i * 2 + (h + 1))
                    pool.nop(nofuse=True)
                    some = pool.value_load(flag[0:1, bass.ds(i * 2 + h, 1)], min_val=0, max_val=HALF * P)
                    with pool.If(some > 0):
                        for t in range(HALF):
                            pool.indirect_dma_start(
                                out=sorted_list,
                                out_offset=bass.IndirectOffsetOnAxis(ap=addr_now[:, h, t:t + 1], axis=0),
                                in_=value_now[:, h, t:t + 1], in_offset=None,
                                bounds_check=STP * P - 1, oob_is_err=False).then_inc(s_scatter[h], 16)
            all_landed = [pool.value_load(landed[0:1, NFLAG + h:NFLAG + h + 1], min_val=16,
                                          max_val=16 + 16 * HALF * (NT // BODY)) for h in range(2)]
            for h in range(2):
                pool.wait_ge(s_scatter[h], all_landed[h])
            pool.sem_inc(s_sorted, 1)

            n = pool.value_load(bodies[0:1, 0:1], min_val=1, max_val=ST // SBODY)
            pool.wait_ge(s_B_stored[0], 16 * ((FQ + 1) // 2))
            pool.wait_ge(s_B_stored[1], 16 * (FQ // 2))
            pool.wait_ge(s_slab_T, FQ + XQ)
            with pool.Fori(0, n) as i:
                for h in range(4):
                    pool.wait_ge(s_receivers, i * 4 + (h + 1))
                    pool.nop(nofuse=True)
                    for k in range(G):
                        pool.indirect_dma_start(
                            out=B_now[:, h, k, :], out_offset=None, in_=B_rows,
                            in_offset=bass.IndirectOffsetOnAxis(ap=dst_now[:, h, k:k + 1], axis=0))\
                            .then_inc(s_gather[h], 16)

            pool.wait_ge(s_sums_done, 1)
            with pool.Fori(0, XQ // 2) as i:
                for k in range(2):
                    pool.wait_ge(s_agg_free, i * 2 + (k + 1))
                    pool.tensor_copy(agg_now[:, k], agg_flat[:, bass.ds(i * (2 * SLAB * D) + k * (SLAB * D), SLAB * D)])\
                        .then_inc(s_agg_now, 1)

        @block.scalar
        def _(act):
            def slab_copies(q, slot, dest_of):
                act.wait_ge(s_slab_T, q + 1)
                for c, w in halves:
                    ins = nc.scalar.copy(slabT[:, slot, c:c + w], bank[4 + c // BANK][:, 0:w])
                ins.then_inc(s_slab_copied, 1)
                act.wait_ge(s_slab_mm, q + 1)
                for c, w in halves:
                    ins = nc.scalar.copy(dest_of(c, w), bank[6 + c // BANK][:, 0:w])
                ins.then_inc(s_slab_out, 1)

            act.wait_ge(s_slab_blank, 1)
            for q in range(FQ):
                if q >= 2:
                    act.wait_ge(s_B_stored[q % 2], 16 * (q // 2))
                slab_copies(q, q % 2, lambda c, w: outs[:, q % 2, c:c + w])
            with act.Fori(0, XQ // 2) as i:
                for k in range(2):
                    slab_copies(i * 2 + (FQ + k), (FQ + k) % 2,
                                lambda c, w: A_flat[:, bass.ds((i * 2 + k) * (SLAB * D) + c, w)])

            act.wait_ge(s_offsets, 1)
            def stage_places(i, h):
                act.wait_ge(s_placed, i * 2 + (h + 1))
                act.wait_ge(s_scatter[h], act.value_load(landed[0:1, bass.ds(i * 2 + h, 1)], min_val=16,
                                                         max_val=16 + 16 * HALF * (NT // BODY)))
                nc.scalar.copy(addr_now[:, h, :], place[:, bass.ds(i * BODY + h * HALF, HALF)])
                nc.scalar.copy(value_now[:, h, :], value[:, bass.ds(i * BODY + h * HALF, HALF)])\
                    .then_inc(s_staged, 1)

            for h in range(2):
                stage_places(0, h)
            with act.Fori(1, NT // BODY) as i:
                for h in range(2):
                    act.wait_ge(s_staged, i * 2 + h)
                    stage_places(i, h)

            act.wait_ge(s_sort_cols, STURNS)
            for h in range(4):
                nc.scalar.copy(dst_now[:, h, :], dst_s[:, G * h:G * h + G]).then_inc(s_receivers, 1)
            n = act.value_load(bodies[0:1, 0:1], min_val=1, max_val=ST // SBODY)
            act.wait_ge(s_sorted, 1)
            with act.Fori(0, n) as i:
                for h in range(4):
                    act.wait_ge(s_oh_turned, i * 4 + (h + 1))
                    act.wait_ge(s_spread, i * 4 + (h + 1))
                    nc.scalar.copy(oh_sT[:, h % 2], bank[3 + h % 2][:]).then_inc(s_oh_copied, 1)
                    act.wait_ge(s_added, i * 4 + (h + 1))
                    act.wait_ge(s_sum_free, i * 4 + (h + 1))
                    nc.scalar.activation(msg[:, h % 2], pre[:, h % 2], ACT.Relu).then_inc(s_msg, 1)
                    nc.scalar.copy(dst_now[:, h, :], dst_s[:, bass.ds(i * SBODY + (SBODY + G * h), G)])\
                        .then_inc(s_receivers, 1)

            def finish(a, slot):
                act.wait_ge(s_x_turned, a + 1)
                for c, w in halves:
                    ins = nc.scalar.copy(slabT[:, 0, c:c + w], bank[3 + c // BANK][:, 0:w])
                ins.then_inc(s_xT, 1)
                act.wait_ge(s_h, a + 1)
                if not (isinstance(a, int) and a == 0):
                    act.wait_ge(s_resid, a)
                for c, w in halves:
                    ins = nc.scalar.activation(slabT[:, 1, c:c + w], bank[1 + c // BANK][:, 0:w], ACT.Relu)
                ins.then_inc(s_relu, 1)
                act.wait_ge(s_var, a + 1)
                nc.scalar.activation(rstd[:, 0, :], mv[:, :, 1], ACT.Sqrt, bias=eps[:, 0:1]).then_inc(s_std, 1)

            for k in range(2):
                finish(k, k)
            with act.Fori(1, XQ // 2) as i:
                for k in range(2):
                    finish(i * 2 + k, k)

        @block.vector
        def _(dve):
            step = [0]

            def link(ins):
                step[0] += 1
                ins.then_inc(s_step, 1)
                dve.wait_ge(s_step, step[0])

            dve.wait_ge(s_edges, 96 if rest else 64)
            link(nc.vector.tensor_scalar(raw_i, edge_raw[:, 0, 0:NT], 7, None, ALU.arith_shift_right))
            link(nc.vector.tensor_copy(edge_row[:, 0, :], raw_i))
            link(nc.vector.tensor_scalar(raw_i, edge_raw[:, 0, 0:NT], 127, None, ALU.bitwise_and))
            nc.vector.tensor_scalar(edge_row[:, 2, :], edge_raw[:, 1, 0:NT], float(LAST), None, ALU.min)
            nc.vector.tensor_copy(edge_row[:, 1, :], raw_i).then_inc(s_rows, 1)

            for g in range(TURNS):
                w = min(BANK, NT - g * BANK)
                cols = slice(g * BANK, g * BANK + w)
                dve.wait_ge(s_turned, g + 1)
                blk, loc, rec = bank[3][:, 0:w], bank[4][:, 0:w], bank[5][:, 0:w]
                nc.vector.tensor_copy(hi_all[:, cols], blk)
                nc.vector.tensor_scalar(value[:, cols], rec, 256.0, None, ALU.mult)
                link(nc.vector.tensor_scalar(place[:, cols], rec, float(LAST), None, ALU.is_ge))
                nc.vector.scalar_tensor_tensor(out=hi_n[:, cols], in0=place[:, cols], scalar=256.0, in1=blk,
                                               op0=ALU.mult, op1=ALU.add)
                nc.vector.scalar_tensor_tensor(out=lo_c[:, cols], in0=place[:, cols], scalar=256.0, in1=loc,
                                               op0=ALU.mult, op1=ALU.add)
                nc.vector.tensor_tensor(value[:, cols], value[:, cols], loc, ALU.add)
                link(nc.vector.tensor_scalar(is_sorted[:, cols], place[:, cols], -1.0, 1.0, ALU.mult, ALU.add))
                nc.vector.tensor_scalar(place[:, cols], place[:, cols], BIG, None, ALU.mult).then_inc(s_cols, 1)
            dve.wait_ge(s_cols, TURNS)
            link(nc.vector.tensor_scalar(lo_c[:], lo_c[:], -256.0, None, ALU.add))

            dve.wait_ge(s_const, 9)

            def onehot_block(t, slot):
                for k in range(G):
                    ins = nc.vector.tensor_scalar(oh_n[:, slot, k, :], iota_hi[:], hi_n[:, bass.ds(t + k, 1)], None,
                                                  ALU.is_equal)
                return ins

            with dve.Fori(0, GROUPS // RING) as i:
                for h in range(RING):
                    dve.wait_ge(s_count_free, i * RING + (h + 1))
                    onehot_block(i * (RING * G) + h * G, h).then_inc(s_count_oh, 1)

            dve.wait_ge(s_count_free, RING + GROUPS)
            link(nc.vector.tensor_copy(count[:].rearrange("p k n -> p (k n)"), counts_ps[:, 0:GW]))
            tot, tiles, ends, zero = small[:, 0], small[:, 1], small[:, 2], small[:, 3]
            link(nc.vector.tensor_tensor(tot, count[:, 0], count[:, 1], ALU.add))
            link(nc.vector.tensor_tensor(tot, tot, count[:, 2], ALU.add))
            link(nc.vector.tensor_tensor(tot, tot, count[:, 3], ALU.add))
            link(nc.vector.tensor_scalar(small_i[:, 0], tot, float(P - 1), None, ALU.add))
            link(nc.vector.tensor_scalar(small_i[:, 1], small_i[:, 0], 7, None, ALU.arith_shift_right))
            nc.vector.memset(zero, 0.0)
            link(nc.vector.tensor_copy(tiles, small_i[:, 1]))
            link(nc.vector.tensor_tensor_scan(ends, tiles, zero, 0.0, ALU.add, ALU.add))
            link(nc.vector.tensor_tensor(start_at[:, 0], ends, tiles, ALU.subtract))
            link(nc.vector.tensor_scalar(start_at[:, 0], start_at[:, 0], float(P), None, ALU.mult))
            for k in range(1, G):
                link(nc.vector.tensor_tensor(start_at[:, k], start_at[:, k - 1], count[:, k - 1], ALU.add))
            link(nc.vector.tensor_scalar(small_i[0:1, 0, 0:1], ends[0:1, NB - 1:NB], float(SBODY - 1), None, ALU.add))
            link(nc.vector.tensor_scalar(small_i[0:1, 0, 1:2], small_i[0:1, 0, 0:1], SBODY.bit_length() - 1, None,
                                         ALU.arith_shift_right))
            nc.vector.tensor_scalar(bodies[:], small_i[0:1, 0, 1:2], 1.0, None, ALU.max)
            dve.wait_ge(s_flags, 1)
            for c in range(TURNS):
                w = min(BANK, NT - c * BANK)
                ins = nc.vector.tensor_reduce(flag_f[0:1, c * BANK // HALF:(c * BANK + w) // HALF],
                                              bank[3 + c][0:1, 0:w].rearrange("p (a b) -> p a b", b=HALF),
                                              AX_X, ALU.add)
            link(ins)
            nc.vector.tensor_copy(flag[:], flag_f[:])
            nc.vector.memset(landed_f[:], 16.0)
            nc.vector.memset(small[0:1, 4, :], 0.0)
            link(nc.vector.tensor_scalar(flag_f[:], flag_f[:], 1.0, float(16 * HALF), ALU.min, ALU.mult))
            for h in range(2):
                ins = nc.vector.tensor_tensor_scan(landed_f[:, 2 + h:2 + NFLAG:2], flag_f[:, h:NFLAG:2],
                                                   small[0:1, 4, 0:NFLAG // 2], 16.0,
                                                   ALU.add, ALU.add)
            link(ins)
            nc.vector.tensor_copy(landed[:], landed_f[:]).then_inc(s_offsets, 1)
            dve.wait_ge(s_ends, 1)
            link(nc.vector.tensor_copy(tile_end[0:NB, 0:1], bank[2][0:NB, 0:1]))
            nc.vector.tensor_scalar(block_le[0:NB, :], tile_iota[0:NB, :], tile_end[0:NB, 0:1], None, ALU.is_ge)\
                .then_inc(s_block_le, 1)
            dve.wait_ge(s_blocks, 1)
            for c in range(STURNS):
                w = min(BANK, STP - c * BANK)
                ins = nc.vector.tensor_scalar(block_of[:, c * BANK:c * BANK + w], bank[3 + c][0:1, 0:w],
                                              float(NB - 1), float(P), ALU.min, ALU.mult)
            ins.then_inc(s_block_of, 1)

            with dve.Fori(0, GROUPS // RING) as i:
                for h in range(RING):
                    t = i * (RING * G) + h * G
                    g1 = i * RING + (h + 1)
                    dve.wait_ge(s_rank_free, g1)
                    onehot_block(t, h).then_inc(s_rank_oh, 1)
                    dve.wait_ge(s_hist_free, g1)
                    for k in range(G):
                        nc.vector.tensor_scalar(oh_lo[:, h % 2, k, :], iota_clamped[:], lo_c[:, bass.ds(t + k, 1)],
                                                None, ALU.is_equal)
                    for k in range(G):
                        ins = nc.vector.tensor_scalar(oh_hi[:, h % 2, k, :], iota_hi[:],
                                                      hi_all[:, bass.ds(t + k, 1)], None, ALU.is_equal)
                    ins.then_inc(s_hist_oh, 1)
                    dve.wait_ge(s_before, g1)
                    for k in range(G):
                        ins = nc.vector.tensor_tensor_reduce(
                            out=count[:, k, :], in0=ranks_ps[:, k * NB:(k + 1) * NB], in1=oh_n[:, h, k, :],
                            scale=1.0, scalar=0.0, op0=ALU.mult, op1=ALU.add,
                            accum_out=rank_now[:, h * G + k:h * G + k + 1])
                    ins.then_inc(s_ranked, 1)
                cols = bass.ds(i * (RING * G), RING * G)
                dve.wait_ge(s_ranked, i * RING + RING)
                nc.vector.tensor_tensor(place[:, cols], place[:, cols], rank_now[:], ALU.add).then_inc(s_placed, 1)

            dve.wait_ge(s_hist_free, 2 + GROUPS)
            link(nc.vector.tensor_copy(clamped_count[:], clamped_ps[:, 0:NB]))
            dve.wait_ge(s_slab_out, 1 + FQ + XQ)
            dve.wait_ge(s_b_last, 16)
            for h in range(2):
                dve.wait_ge(s_scatter[h], 16)
            with dve.Fori(0, NB // SLAB) as j:
                for t in range(SLAB):
                    cols = bass.ds(j * (SLAB * D) + t * D, D)
                    ins = nc.vector.tensor_tensor(agg_flat[:, cols], A_flat[:, cols], b_last[:], ALU.add)
                ins.then_inc(s_clamped_add, 1)
                dve.wait_ge(s_clamped_add, j + 1)
                for t in range(SLAB):
                    cols = bass.ds(j * (SLAB * D) + t * D, D)
                    ins = nc.vector.tensor_scalar(agg_flat[:, cols], agg_flat[:, cols], 0.0,
                                                  clamped_count[:, bass.ds(j * SLAB + t, 1)], ALU.max, ALU.mult)
            ins = nc.vector.memset(small[:, 3], 0.0)
            link(ins)

            for c in range(STURNS):
                w = min(BANK, STP - c * BANK)
                cols = slice(c * BANK, c * BANK + w)
                dve.wait_ge(s_sort_turned, 1)
                link(nc.vector.tensor_copy(sort_i[:, 0:w], bank[3 + c][:, 0:w]))
                nc.vector.tensor_scalar(sort_d[:, 0:w], sort_i[:, 0:w], 8, None, ALU.arith_shift_right)
                link(nc.vector.tensor_scalar(sort_l[:, 0:w], sort_i[:, 0:w], 255, None, ALU.bitwise_and))
                nc.vector.tensor_copy(dst_s[:, cols], sort_d[:, 0:w])
                ins = nc.vector.tensor_copy(lo_s[:, cols], sort_l[:, 0:w])
                ins.then_inc(s_sort_cols, 1)
                dve.wait_ge(s_sort_cols, c + 1)

            dve.sem_inc(s_agg, 1)
            n = dve.value_load(bodies[0:1, 0:1], min_val=1, max_val=ST // SBODY)
            with dve.Fori(0, n) as i:
                for h in range(4):
                    g1 = i * 4 + (h + 1)
                    dve.wait_ge(s_sum_free, g1)
                    for k in range(G):
                        ins = nc.vector.tensor_scalar(oh_s[:, h % 2, k * P:(k + 1) * P], iota_lo[:],
                                                      lo_s[:, bass.ds(i * SBODY + (G * h + k), 1)], None, ALU.is_equal)
                    ins.then_inc(s_oh_s, 1)
                    dve.wait_ge(s_spread, g1 + 2)
                    dve.wait_ge(s_gather[h], i * (16 * G) + 16 * G)
                    nc.vector.tensor_tensor(pre[:, h % 2], bank[5 + h % 2][:],
                                            B_now[:, h].rearrange("p k n -> p (k n)"), ALU.add).then_inc(s_added, 1)
                    dve.wait_ge(s_sum_free, g1 + 2)
                    for k in range(G):
                        b = dve.value_load(block_of[:, bass.ds(i * SBODY + (G * h + k), 1)],
                                           min_val=0, max_val=(NB - 1) * P)
                        dve.wait_ge(s_agg, i * SBODY + (G * h + k + 1))
                        nc.vector.tensor_tensor(agg_flat[:, bass.ds(b, D)], agg_flat[:, bass.ds(b, D)],
                                                bank[7 * (h % 2)][:, k * D:(k + 1) * D], ALU.add)\
                            .then_inc(s_agg, 1)
            nc.vector.memset(small[:, 3], 0.0).then_inc(s_sums_done, 1)

            def finish(a, slot):
                dve.wait_ge(s_agg_free, a + 3)
                for c, w in halves:
                    ins = nc.vector.tensor_copy(aggT[:, c:c + w], bank[5 + c // BANK][:, 0:w])
                ins.then_inc(s_aT, 1)
                dve.wait_ge(s_relu, a + 1)
                nc.vector.scalar_tensor_tensor(out=resid, in0=slab[:, slot], scalar=2.0, in1=slabT[:, 1, :],
                                               op0=ALU.mult, op1=ALU.add).then_inc(s_resid, 1)
                dve.wait_ge(s_resid, a + 1)
                for t in range(SLAB):
                    ins = nc.vector.bn_stats(stats[:, t, :], resid[:, t * D:(t + 1) * D])
                ins.then_inc(s_stats, 1)
                dve.wait_ge(s_stats, a + 1)
                dve.nop(nofuse=True)
                for t in range(SLAB):
                    ins = nc.vector.bn_aggr(mv[:, t, :], stats[:, t, :])
                ins.then_inc(s_var, 1)
                dve.wait_ge(s_std, a + 1)
                nc.vector.reciprocal(rstd[:, 1, :], rstd[:, 0, :]).then_inc(s_recip, 1)
                dve.wait_ge(s_recip, a + 1)
                for t in range(SLAB):
                    ins = nc.vector.tensor_scalar(outs[:, slot, t * D:(t + 1) * D], resid[:, t * D:(t + 1) * D],
                                                  mv[:, t, 0:1], rstd[:, 1, t:t + 1], ALU.subtract, ALU.mult)
                ins.then_inc(s_y, 1)

            for k in range(2):
                finish(k, k)
            with dve.Fori(1, XQ // 2) as i:
                for k in range(2):
                    dve.wait_ge(s_out[k], i * 32)
                    finish(i * 2 + k, k)

        @block.tensor
        def _(pe):
            pe.wait_ge(s_const, 9)
            pe.wait_ge(s_rows, 1)
            for g in range(TURNS):
                if g:
                    pe.wait_ge(s_cols, g)
                for k in range(3):
                    for c in range(min(4, CH - 4 * g)):
                        col = (4 * g + c) * P
                        ins = nc.tensor.transpose(bank[3 + k][:, c * P:(c + 1) * P], edge_row[:, k, col:col + P],
                                                  ident[:])
                ins.then_inc(s_turned, 1)
            pe.wait_ge(s_cols, TURNS)

            def turn_tile(slot, t):
                return nc.tensor.transpose(bank[4 + t // 4][:, t % 4 * P:(t % 4 + 1) * P],
                                           slab[:, slot, t * D:(t + 1) * D], ident[:])

            def multiply_tile(slot, t, half):
                to = bank[6 + t // 4][:, t % 4 * D:(t % 4 + 1) * D]
                ins = nc.tensor.matmul(to, slabT[:, slot, t * P:(t + 1) * P], wm[:, half, :],
                                       start=True, stop=(half == 1))
                if half == 0:
                    ins = nc.tensor.matmul(to, ones_f[0:1, :], bm_row[:], start=False, stop=True)
                return ins

            def count_body(b, q, half, loads):
                for g in range(CBODY):
                    pe.wait_ge(s_count_oh, b * CBODY + (g + 1))
                    nc.tensor.matmul(counts_ps[:, 0:GW], ones_bf[:], oh_n[:, g % RING].rearrange("p k n -> p (k n)"),
                                     start=False, stop=False, skip_group_check=True).then_inc(s_count_free, 1)
                    if half is None:
                        continue
                    slot = q[1]
                    if g == 0:
                        pe.wait_ge(s_slab[slot], loads)
                        pe.wait_ge(s_slab_copied, q[0] + 1)
                    if g < 4:
                        for t in range(2 * g, min(2 * g + 2, SLAB)):
                            ins = turn_tile(slot, t)
                        if g == 3:
                            ins.then_inc(s_slab_T, 1)
                    if g == CBODY - SLAB:
                        pe.wait_ge(s_slab_copied, q[0] + 2)
                        pe.wait_ge(s_slab_out, q[0] + 1)
                    if g >= CBODY - SLAB:
                        ins = multiply_tile(slot, g - (CBODY - SLAB), half)
                        if g == CBODY - 1:
                            ins.then_inc(s_slab_mm, 1)

            pe.wait_ge(s_weights, 64)
            nc.tensor.matmul(counts_ps[:, 0:GW], zeros_bf[:, 0:P], zeros_bf[:], start=True, stop=False,
                             skip_group_check=True).then_inc(s_zeroed, 1)
            pe.sem_inc(s_count_free, RING)
            pe.sem_inc(s_slab_copied, 1)
            pe.sem_inc(s_slab_out, 1)
            with pe.Fori(0, FQ // 2) as i:
                for k in range(2):
                    count_body(i * 2 + k, (i * 2 + k, k), 1, i * 32 + 32)
            count_body(FQ - 1, (FQ - 1, 0), 1, 32 * ((FQ + 1) // 2))
            count_body(FQ, (FQ, 1), 0, 32 * ((FQ + 1) // 2))
            with pe.Fori((FQ + 1) // 2, (FQ + XQ) // 2) as i:
                for k in range(2):
                    count_body(i * 2 + k, (i * 2 + k, k), 0, i * 32 + 32)
            count_body(FQ + XQ - 1, (FQ + XQ - 1, 0), 0, 32 * ((FQ + XQ + 1) // 2))
            with pe.Fori(FQ + XQ, GROUPS // CBODY) as b:
                count_body(b, None, None, None)

            pe.wait_ge(s_slab_out, 1 + FQ + XQ)
            for c in range(TURNS):
                w = min(BANK, NT - c * BANK)
                ins = nc.tensor.matmul(bank[3 + c][0:1, 0:w], ones_f[:, 0:1], is_sorted[:, c * BANK:c * BANK + w],
                                       start=True, stop=True)
            ins.then_inc(s_flags, 1)
            pe.wait_ge(s_offsets, 1)
            nc.tensor.transpose(bank[2][0:NB, 0:P], small[:, 2, :], ident[:]).then_inc(s_ends, 1)
            nc.tensor.matmul(ranks_ps[:, 0:GW], ident[:], start_at[:].rearrange("p k n -> p (k n)"),
                             start=True, stop=False, skip_group_check=True)
            pe.wait_ge(s_block_le, 1)
            for c in range(STURNS):
                w = min(BANK, STP - c * BANK)
                ins = nc.tensor.matmul(bank[3 + c][0:1, 0:w], ones_f[0:NB, 0:1], block_le[0:NB, c * BANK:c * BANK + w],
                                       start=True, stop=True)
            ins.then_inc(s_blocks, 1)

            nc.tensor.matmul(clamped_ps[:, 0:NB], zeros_bf[:, 0:P], zeros_bf[:, 0:NB], start=True, stop=False,
                             skip_group_check=True).then_inc(s_zeroed, 1)
            pe.sem_inc(s_rank_free, RING)
            pe.sem_inc(s_hist_free, 2)
            with pe.Fori(0, GROUPS // RING) as i:
                for h in range(RING):
                    g1 = i * RING + (h + 1)
                    onehots = oh_n[:, h].rearrange("p k n -> p (k n)")
                    pe.wait_ge(s_rank_oh, g1)
                    nc.tensor.matmul(ranks_ps[:, 0:GW], before[:], onehots, start=False, stop=False,
                                     skip_group_check=True).then_inc(s_before, 1)
                    pe.wait_ge(s_hist_oh, g1)
                    for k in range(G):
                        ins = nc.tensor.matmul(clamped_ps[:, 0:NB], oh_lo[:, h % 2, k, :], oh_hi[:, h % 2, k, :],
                                               start=False, stop=False, skip_group_check=True)
                    ins.then_inc(s_hist_free, 1)
                    pe.wait_ge(s_ranked, g1)
                    nc.tensor.matmul(ranks_ps[:, 0:GW], from_on[:], onehots, start=False, stop=False,
                                     skip_group_check=True).then_inc(s_rank_free, 1)

            pe.wait_ge(s_list_back, 16)
            pe.wait_ge(s_block_of, 1)
            for c in range(SCH):
                ins = nc.tensor.transpose(bank[3 + c // 4][:, c % 4 * P:(c % 4 + 1) * P],
                                          sorted_rows[:, c * P:(c + 1) * P], ident[:])
            ins.then_inc(s_sort_turned, 1)

            n = pe.value_load(bodies[0:1, 0:1], min_val=1, max_val=ST // SBODY)
            pe.sem_inc(s_spread, 2)
            pe.sem_inc(s_sum_free, 2)
            pe.wait_ge(s_sort_cols, STURNS)

            def turn_and_spread(i, h):
                g1 = i * 4 + (h + 1)
                pe.wait_ge(s_oh_s, g1)
                for k in range(G):
                    ins = nc.tensor.transpose(bank[3 + h % 2][:, k * P:(k + 1) * P],
                                              oh_s[:, h % 2, k * P:(k + 1) * P], ident[:])
                ins.then_inc(s_oh_turned, 1)
                blocks = [pe.value_load(block_of[:, bass.ds(i * SBODY + (G * h + k), 1)],
                                        min_val=0, max_val=(NB - 1) * P) for k in range(G)]
                pe.wait_ge(s_oh_copied, g1)
                for k in range(G):
                    ins = nc.tensor.matmul(bank[5 + h % 2][:, k * D:(k + 1) * D], oh_sT[:, h % 2, k * P:(k + 1) * P],
                                           A_flat[:, bass.ds(blocks[k], D)], start=True, stop=True)
                ins.then_inc(s_spread, 1)

            def sum_messages(i, h):
                g1 = i * 4 + (h + 1)
                pe.wait_ge(s_msg, g1)
                for k in range(G):
                    ins = nc.tensor.matmul(bank[7 * (h % 2)][:, k * D:(k + 1) * D],
                                           oh_s[:, h % 2, k * P:(k + 1) * P], msg[:, h % 2, k * D:(k + 1) * D],
                                           start=True, stop=True)
                ins.then_inc(s_sum_free, 1)

            with pe.Fori(0, n) as i:
                for h in range(4):
                    turn_and_spread(i, h)
                    sum_messages(i, h)

            def finish(a, slot, loads):
                pe.wait_ge(s_x[slot], loads)
                later = not (isinstance(a, int) and a == 0)
                if later:
                    pe.wait_ge(s_xT, a)
                for t in range(SLAB):
                    ins = nc.tensor.transpose(bank[3 + t // 4][:, t % 4 * P:(t % 4 + 1) * P],
                                              slab[:, slot, t * D:(t + 1) * D], ident[:])
                ins.then_inc(s_x_turned, 1)
                if later:
                    pe.wait_ge(s_aT, a)
                pe.wait_ge(s_agg_now, a + 1)
                for t in range(SLAB):
                    ins = nc.tensor.transpose(bank[5 + t // 4][:, t % 4 * P:(t % 4 + 1) * P],
                                              agg_now[:, slot, t * D:(t + 1) * D], ident[:])
                ins.then_inc(s_agg_free, 1)
                if later:
                    pe.wait_ge(s_relu, a)
                pe.wait_ge(s_xT, a + 1)
                pe.wait_ge(s_aT, a + 1)
                for t in range(SLAB):
                    to = bank[1 + t // 4][:, t % 4 * D:(t % 4 + 1) * D]
                    nc.tensor.matmul(to, slabT[:, 0, t * P:(t + 1) * P], wc[:, 0, :], start=True, stop=False)
                    nc.tensor.matmul(to, aggT[:, t * P:(t + 1) * P], wc[:, 1, :], start=False, stop=False)
                    ins = nc.tensor.matmul(to, ones_f[0:1, :], bc_row[:], start=False, stop=True)
                ins.then_inc(s_h, 1)

            pe.wait_ge(s_sums_done, 1)
            pe.sem_inc(s_agg_free, 2)
            for k in range(2):
                finish(k, k, 32)
            with pe.Fori(1, XQ // 2) as i:
                for k in range(2):
                    finish(i * 2 + k, k, i * 32 + 32)


_INS = ["x", "src", "dst", "L0_gnn_factors", "L0_gnn_Wm", "L0_gnn_bm", "L0_gnn_Wc", "L0_gnn_bc"]


def kernel(**inputs):
    import numpy as _np
    import concourse.bacc as _bacc
    from concourse import mybir as _mybir
    from concourse.bass_utils import run_bass_kernel_spmd as _run

    nc = _bacc.Bacc("TRN2", target_bir_lowering=False, num_devices=1)
    arrays, args = {}, []
    for name in _INS:
        a = _np.ascontiguousarray(inputs[name])
        arrays[f"in_{name}_dram"] = a
        args.append(nc.dram_tensor(f"in_{name}_dram", a.shape, _mybir.dt.from_np(a.dtype), kind="ExternalInput").ap())
    shape = inputs["x"].shape
    args.append(nc.dram_tensor("out_dram", shape, _mybir.dt.float32, kind="ExternalOutput").ap())
    gnn_kernel(nc, *args)
    r = _run(nc, [arrays], core_ids=[0])
    return r.results[0]["out_dram"]
```

```python
from contextlib import ExitStack

import concourse.bass as bass
from concourse import mybir

ALU = mybir.AluOpType
ACT = mybir.ActivationFunctionType
F32 = mybir.dt.float32
BF16 = mybir.dt.bfloat16
I32 = mybir.dt.int32
AX_X = mybir.AxisListType.X

P = 128
C = 16
G = 4
BIG = float(1 << 20)
BLANK = 128
BANK = 512
SLAB = 7
IN_TABLE = "the table holds block * 128 with block clamped to the last one"


def gnn_kernel(nc, x, src, dst, factors, Wm, bm, Wc, bc, out):
    N, D = x.shape
    F = factors.shape[0]
    E = src.shape[0]
    LAST = F - 1
    NB = -(-N // P)
    FB = -(-F // P)
    NTAIL, FTAIL = N - (NB - 1) * P, F - (FB - 1) * P
    CH = -(-E // (P * P))
    NT = CH * P
    ROUNDS = NT // C
    HALF = ROUNDS // 2
    full_rows = (E - (CH - 1) * P * P) // P
    rest = E - (CH - 1) * P * P - full_rows * P
    ST = -(-(-(-E // P) + NB) // C) * C
    SCH = -(-(ST + C) // P)
    STP = SCH * P
    GW = G * NB
    FQ = FB // SLAB
    XQ = NB // SLAB
    TURNS = -(-CH // 4)
    STURNS = -(-SCH // 4)
    PARTS = [(0, 4), (4, 3)]
    SD = SLAB * D
    LANDED_MAX = 16 + 16 * C * (HALF // 2)
    assert D == P and GW <= BANK and ROUNDS % 4 == 0 and NB % SLAB == 0 and FB % SLAB == 0 and XQ % 2 == 0
    assert FQ == 7 and HALF > XQ and STP * P < BIG and STP * 7 <= NB * D

    sorted_list = nc.dram_tensor("sorted_list", (STP * P, 1), F32).ap()
    B_rows = nc.dram_tensor("B_rows", (FB * P, D), F32).ap()
    H_rows = nc.dram_tensor("H_rows", (NB * P, D), F32).ap()

    with ExitStack() as ctx:
        def sb(name, shape, dt=F32):
            return ctx.enter_context(nc.sbuf_tensor(name, shape, dt))

        def sem(name):
            return ctx.enter_context(nc.semaphore(name))

        bank = [ctx.enter_context(nc.psum_tensor(f"bank{i}", [P, BANK], F32)) for i in range(8)]

        ident = sb("ident", [P, P])
        ident_bf = sb("ident_bf", [P, P], BF16)
        before = sb("before", [P, P], BF16)
        from_on = sb("from_on", [P, P], BF16)
        ones_bf = sb("ones_bf", [P, P], BF16)
        ones_f = sb("ones_f", [P, P])
        zeros_bf = sb("zeros_bf", [P, GW], BF16)
        iota_hi = sb("iota_hi", [P, NB, C], BF16)
        iota_lo = sb("iota_lo", [P, P, C], BF16)
        eps = sb("eps", [P, 1])
        wm = sb("wm", [P, 2, D])
        wc = sb("wc", [P, 2, D])
        bm_row = sb("bm_row", [1, D])
        bc_row = sb("bc_row", [1, D])
        b_last = sb("b_last", [3, D])
        b_left = sb("b_left", [3, 2, D])
        b_split = sb("b_split", [3, 3, D], BF16)
        b_parts = sb("b_parts", [3, D], BF16)

        agg = sb("agg", [P, NB, D])
        A_high = sb("A_high", [P, 2, NB * D], BF16)
        row_mem = sb("row_mem", [P, 2 * STP + 3 * NT])
        col_mem = sb("col_mem", [P, 9200])
        stage = sb("stage", [P, 4 * SD])
        turned = sb("turned", [P, 2, BANK])

        small = sb("small", [P, 6, NB])
        small_i = sb("small_i", [P, 2, NB], I32)
        tile_end = sb("tile_end", [P, 1])
        flag = sb("flag", [1, ROUNDS], I32)
        flag_f = sb("flag_f", [1, ROUNDS])
        landed_f = sb("landed_f", [1, 2, HALF + 2])
        landed = sb("landed", [1, 2, HALF + 2], I32)
        bodies = sb("bodies", [1, 1], I32)
        addr_now = sb("addr_now", [P, 4, C], I32)
        value_now = sb("value_now", [P, 4, C])
        rank_now = sb("rank_now", [P, C])
        dst_now = sb("dst_now", [P, 4, G], I32)
        clamped_count = sb("clamped_count", [P, NB])
        stats = sb("stats", [P, SLAB, 6])
        mv = sb("mv", [P, SLAB, 2])
        rstd = sb("rstd", [P, 3, SLAB])

        agg_flat = agg[:].rearrange("p a b -> p (a b)")
        blank_fill = agg_flat[:, 0:STP // 4]
        r1 = agg_flat[:, STP // 2:STP // 2 + BANK]
        block_le = agg_flat[:, STP:2 * STP]
        tile_iota = agg_flat[:, 2 * STP:3 * STP]
        is_sorted = agg_flat[:, 3 * STP:3 * STP + NT]
        count = agg_flat[:, 4 * STP:4 * STP + NB * C].rearrange("p (b t) -> p b t", t=C)
        start_at = agg_flat[:, 5 * STP:5 * STP + NB * C].rearrange("p (b t) -> p b t", t=C)
        edge_raw = row_mem[:, 0:2 * STP].bitcast(I32).rearrange("p (k t) -> p k t", k=2)
        edge_row = row_mem[:, 2 * STP:2 * STP + 3 * NT].rearrange("p (k t) -> p k t", k=3)
        A_low = row_mem[:, 0:NB * D // 2].bitcast(BF16)
        A_parts = [A_high[:, 0, :], A_high[:, 1, :], A_low]
        TAB = NB * D // 2
        block_of = row_mem[0:1, TAB:TAB + G + STP].bitcast(I32)
        assert TAB + G + STP <= 2 * STP + 3 * NT
        off = [0]

        def carve(words):
            off[0] += words
            return col_mem[:, off[0] - words:off[0]]

        value = carve(NT)
        place = carve(NT)
        hi_n = carve(NT // 2).bitcast(BF16)
        hi_all = carve(NT // 2).bitcast(BF16)
        lo_c = carve(NT // 2).bitcast(BF16)
        oh_n = carve(NB * C).bitcast(BF16).rearrange("p (s b t) -> p s b t", s=2, t=C)
        oh_lo = carve(P * C // 2).bitcast(BF16).rearrange("p (n t) -> p n t", t=C)
        oh_hi = carve(NB * C // 2).bitcast(BF16).rearrange("p (b t) -> p b t", t=C)
        assert off[0] <= 9200
        off[0] = 0
        sorted_rows = carve(STP)
        dst_s = carve(STP).bitcast(I32)
        lo_s = carve(STP // 2).bitcast(BF16)
        oh_s = carve(4 * P * G // 2).bitcast(BF16).rearrange("p (s n k) -> p s n k", s=4, k=G)
        oh32 = carve(2 * P * G).rearrange("p (s k n) -> p s k n", s=2, k=G)
        msg = carve(2 * G * D).rearrange("p (s m) -> p s m", s=2)
        sort_i = carve(BANK).bitcast(I32)
        sort_l = carve(BANK).bitcast(I32)
        pre = sorted_rows[:, 0:2 * G * D].rearrange("p (s m) -> p s m", s=2)
        oh_sT = turned[:, 0, :].bitcast(BF16).rearrange("p (s m) -> p s m", s=2)
        assert off[0] <= 9200 and 2 * G * D <= STP
        slab = stage[:, 0:2 * SD].rearrange("p (s m) -> p s m", s=2)
        outs = stage[:, 2 * SD:4 * SD].rearrange("p (s m) -> p s m", s=2)
        B_now = stage[:, 0:4 * G * D].rearrange("p (s k d) -> p s k d", s=4, k=G)
        late = A_high[:].rearrange("p k m -> p (k m)").bitcast(F32)
        agg_now, aggT, H_now, hid, resid = [late[:, 2 * SD * k:2 * SD * (k + 1)].rearrange("p (s m) -> p s m", s=2)
                                            for k in range(5)]

        fac_tiles = factors[0:(FB - 1) * P].rearrange("(t p) d -> p t d", p=P)
        x_tiles = x[0:(NB - 1) * P].rearrange("(t p) d -> p t d", p=P)
        out_tiles = out[0:(NB - 1) * P].rearrange("(t p) d -> p t d", p=P)
        B_tiles = B_rows.rearrange("(t p) d -> p t d", p=P)
        H_tiles = H_rows.rearrange("(t p) d -> p t d", p=P)
        halves = [(0, BANK), (BANK, SD - BANK)]

        s_blank_edges = sem("s_blank_edges")
        s_edges = sem("s_edges")
        s_weights = sem("s_weights")
        s_slab_blank = sem("s_slab_blank")
        s_slab = [sem(f"s_slab{k}") for k in range(2)]
        s_part_turned = sem("s_part_turned")
        s_rows_out = sem("s_rows_out")
        s_stored = [sem(f"s_stored{k}") for k in range(2)]
        s_b_last = sem("s_b_last")
        s_sorted = sem("s_sorted")
        s_list_back = [sem(f"s_list_back{k}") for k in range(4)]
        s_sums_done = sem("s_sums_done")
        s_x = [sem(f"s_x{k}") for k in range(2)]
        s_y = sem("s_y")
        s_out = [sem(f"s_out{k}") for k in range(2)]
        s_ones = sem("s_ones")
        s_const = sem("s_const")
        s_blank_fill = sem("s_blank_fill")
        s_scatter = [sem(f"s_scatter{k}") for k in range(4)]
        s_tables = sem("s_tables")
        s_staged = sem("s_staged")
        s_receivers = sem("s_receivers")
        s_gather = [sem(f"s_gather{k}") for k in range(4)]
        s_agg_turned = sem("s_agg_turned")
        s_agg_now = sem("s_agg_now")
        s_part_copied = sem("s_part_copied")
        s_products = sem("s_products")
        s_high = sem("s_high")
        s_r1 = sem("s_r1")
        s_mid = sem("s_mid")
        s_placed = sem("s_placed")
        s_counted = sem("s_counted")
        s_clamped_sum = sem("s_clamped_sum")
        s_clamped_act = sem("s_clamped_act")
        s_sort_cols = sem("s_sort_cols")
        s_oh_turned = sem("s_oh_turned")
        s_oh_copied = sem("s_oh_copied")
        s_summed = sem("s_summed")
        s_added = sem("s_added")
        s_msg = sem("s_msg")
        s_aT = sem("s_aT")
        s_hidden = sem("s_hidden")
        s_relu = sem("s_relu")
        s_var = sem("s_var")
        s_std = sem("s_std")
        s_step = sem("s_step")
        s_rows = sem("s_rows")
        s_turned = sem("s_turned")
        s_cols = sem("s_cols")
        s_count_free = sem("s_count_free")
        s_count_oh = sem("s_count_oh")
        s_starts = sem("s_starts")
        s_flags = sem("s_flags")
        s_ends = sem("s_ends")
        s_block_le = sem("s_block_le")
        s_blocks = sem("s_blocks")
        s_block_of = sem("s_block_of")
        s_b_parts = sem("s_b_parts")
        s_rank_free = sem("s_rank_free")
        s_rank_oh = sem("s_rank_oh")
        s_hist_free = sem("s_hist_free")
        s_hist_oh = sem("s_hist_oh")
        s_before = sem("s_before")
        s_ranked = sem("s_ranked")
        s_low = sem("s_low")
        s_clamped_dve = sem("s_clamped_dve")
        s_sort_turned = sem("s_sort_turned")
        s_agg = sem("s_agg")
        s_oh_s = sem("s_oh_s")
        s_spread = sem("s_spread")
        s_h = sem("s_h")
        s_resid = sem("s_resid")
        s_stats = sem("s_stats")
        s_recip = sem("s_recip")
        s_zeroed = sem("s_zeroed")
        block = ctx.enter_context(nc.Block())

        def by_tile(slab_ap):
            return slab_ap.rearrange("p (t d) -> p t d", d=D)

        def load_slab(eng, dest, tiles, whole, a, tail, semaphore, last):
            dest = by_tile(dest)
            if not last:
                eng.dma_start(dest, tiles[:, bass.ds(a * SLAB, SLAB), :]).then_inc(semaphore, 32)
                return
            first = a * SLAB
            eng.dma_start(dest[:, 0:SLAB - 1, :], tiles[:, first:first + SLAB - 1, :]).then_inc(semaphore, 16)
            eng.dma_start(dest[0:tail, SLAB - 1, :], whole[(first + SLAB - 1) * P:, :]).then_inc(semaphore, 16)

        @block.sync
        def _(sp):
            sp.wait_ge(s_blank_edges, 1)
            for k, edges in enumerate((src, dst)):
                whole = edges[0:(CH - 1) * P * P].rearrange("(c r e) -> r c e", r=P, e=P)
                sp.dma_start(edge_raw[:, k, 0:(CH - 1) * P].rearrange("r (c e) -> r c e", e=P), whole)\
                    .then_inc(s_edges, 16)
                part = edges[(CH - 1) * P * P:E - rest].rearrange("(r e) -> r e", e=P)
                sp.dma_start(edge_raw[0:full_rows, k, (CH - 1) * P:NT], part).then_inc(s_edges, 16)
                if rest:
                    sp.dma_start(edge_raw[full_rows:full_rows + 1, k, (CH - 1) * P:(CH - 1) * P + rest],
                                 edges[E - rest:E].rearrange("(a e) -> a e", a=1)).then_inc(s_edges, 16)
            sp.dma_start(wm[:], Wm.rearrange("(k p) n -> p k n", p=P)).then_inc(s_weights, 16)
            sp.dma_start(wc[:], Wc.rearrange("(k p) n -> p k n", p=P)).then_inc(s_weights, 16)
            sp.dma_start(bm_row[:], bm.rearrange("(a d) -> a d", a=1)).then_inc(s_weights, 16)
            sp.dma_start(bc_row[:], bc.rearrange("(a d) -> a d", a=1)).then_inc(s_weights, 16)
            sp.wait_ge(s_slab_blank, 1)
            load_slab(sp, slab[:, 0], fac_tiles, factors, 0, FTAIL, s_slab[0], False)
            load_slab(sp, slab[:, 1], fac_tiles, factors, 1, FTAIL, s_slab[1], False)

            for q in range(FQ):
                n = q + 2
                sp.wait_ge(s_part_turned, 2 * q + 2)
                if n < FQ:
                    load_slab(sp, slab[:, n % 2], fac_tiles, factors, n, FTAIL, s_slab[n % 2], n == FQ - 1)
                else:
                    load_slab(sp, slab[:, n % 2], x_tiles, x, n - FQ, NTAIL, s_slab[n % 2], False)
                sp.wait_ge(s_rows_out, 2 * q + 3)
                sp.dma_start(B_tiles[:, q * SLAB:(q + 1) * SLAB, :], by_tile(outs[:, q % 2]))\
                    .then_inc(s_stored[q % 2], 16)
            sp.wait_ge(s_stored[0], 16 * ((FQ + 1) // 2))
            sp.wait_ge(s_stored[1], 16 * (FQ // 2))
            for k in range(3):
                sp.dma_start(b_last[k:k + 1, :], B_rows[LAST:LAST + 1, :]).then_inc(s_b_last, 16)

            def next_x(a, k, last):
                slot = (FQ + k) % 2
                sp.wait_ge(s_part_turned, a * 2 + (2 * FQ + 2))
                if last is not None:
                    load_slab(sp, slab[:, slot], x_tiles, x, a + 2, NTAIL, s_slab[slot], last)
                sp.wait_ge(s_rows_out, a * 2 + (2 * FQ + 3))
                sp.dma_start(H_tiles[:, bass.ds(a * SLAB, SLAB), :], by_tile(outs[:, slot]))\
                    .then_inc(s_stored[slot], 16)

            with sp.Fori(0, XQ // 2 - 2) as i:
                for k in range(2):
                    next_x(i * 2 + k, k, False)
            for a in range(XQ - 4, XQ):
                next_x(a, a % 2, a + 2 == XQ - 1 if a + 2 < XQ else None)

            sp.wait_ge(s_sorted, 1)
            for c in range(STURNS):
                w = min(4, SCH - 4 * c)
                sp.dma_start(sorted_rows[:, c * BANK:c * BANK + w * P].rearrange("r (c e) -> r c e", e=P),
                             sorted_list[c * 4 * P * P:(c * 4 + w) * P * P]
                             .rearrange("(c r e) a -> r c (e a)", r=P, e=P)).then_inc(s_list_back[c], 16)

            sp.wait_ge(s_stored[0], 16 * ((FQ + XQ + 1) // 2))
            sp.wait_ge(s_stored[1], 16 * ((FQ + XQ) // 2))
            sp.wait_ge(s_sums_done, 1)

            def load_last(a, slot, last):
                load_slab(sp, slab[:, slot], x_tiles, x, a, NTAIL, s_x[slot], last)
                sp.dma_start(by_tile(H_now[:, slot]), H_tiles[:, bass.ds(a * SLAB, SLAB), :]).then_inc(s_x[slot], 16)

            def store_out(a, slot, last):
                sp.wait_ge(s_y, a + 1)
                rows = by_tile(outs[:, slot])
                if not last:
                    sp.dma_start(out_tiles[:, bass.ds(a * SLAB, SLAB), :], rows).then_inc(s_out[slot], 32)
                else:
                    sp.dma_start(out_tiles[:, a * SLAB:a * SLAB + SLAB - 1, :], rows[:, 0:SLAB - 1, :])\
                        .then_inc(s_out[slot], 16)
                    sp.dma_start(out[(NB - 1) * P:N, :], rows[0:NTAIL, SLAB - 1, :]).then_inc(s_out[slot], 16)

            load_last(0, 0, False)
            load_last(1, 1, False)
            with sp.Fori(0, (XQ - 4) // 2) as i:
                for k in range(2):
                    store_out(i * 2 + k, k, False)
                    load_last(i * 2 + (2 + k), k, False)
            for a in range(XQ - 4, XQ):
                store_out(a, a % 2, a == XQ - 1)
                if a + 2 < XQ:
                    load_last(a + 2, a % 2, a + 2 == XQ - 1)
            for k in range(2):
                sp.wait_ge(s_out[k], 32 * (XQ // 2))

        @block.gpsimd
        def _(pool):
            pool.memset(edge_raw[:, :, (CH - 1) * P:NT], 32767).then_inc(s_blank_edges, 1)
            pool.memset(stage[:], 0.0).then_inc(s_slab_blank, 1)
            pool.memset(ones_f[:], 1.0).then_inc(s_ones, 1)
            pool.memset(ones_bf[:], 1.0).then_inc(s_ones, 1)
            pool.wait_ge(s_ones, 2)
            pool.affine_select(out=ident[:], in_=ones_f[:], compare_op=ALU.is_equal, fill=0.0, base=0,
                               pattern=[[1, P]], channel_multiplier=-1).then_inc(s_const, 1)
            pool.affine_select(out=ident_bf[:], in_=ones_bf[:], compare_op=ALU.is_equal, fill=0.0, base=0,
                               pattern=[[1, P]], channel_multiplier=-1).then_inc(s_const, 1)
            pool.iota(iota_hi[:], [[1, NB], [0, C]], base=0, channel_multiplier=0,
                      allow_small_or_imprecise_dtypes=True).then_inc(s_const, 1)
            pool.memset(zeros_bf[:], 0.0).then_inc(s_const, 1)
            pool.iota(iota_lo[:], [[1, P], [0, C]], base=0, channel_multiplier=0,
                      allow_small_or_imprecise_dtypes=True).then_inc(s_const, 1)
            pool.affine_select(out=before[:], in_=ones_bf[:], compare_op=ALU.is_gt, fill=0.0, base=0,
                               pattern=[[1, P]], channel_multiplier=-1).then_inc(s_const, 1)
            pool.affine_select(out=from_on[:], in_=ones_bf[:], compare_op=ALU.is_ge, fill=0.0, base=0,
                               pattern=[[-1, P]], channel_multiplier=1).then_inc(s_const, 1)
            pool.memset(eps[:], 1e-5).then_inc(s_const, 1)
            pool.iota(tile_iota, [[1, STP]], base=0, channel_multiplier=0,
                      allow_small_or_imprecise_dtypes=True).then_inc(s_const, 1)
            pool.memset(blank_fill, float(BLANK)).then_inc(s_blank_fill, 1)

            pool.wait_ge(s_blank_fill, 1)
            for h in range(4):
                rows = slice(h * (STP * P // 4), (h + 1) * (STP * P // 4))
                pool.dma_start(sorted_list[rows].rearrange("(p n) a -> p (n a)", p=P), blank_fill)\
                    .then_inc(s_scatter[h], 16)
            for h in range(4):
                pool.wait_ge(s_scatter[h], 16)

            pool.wait_ge(s_tables, 1)
            with pool.Fori(0, HALF // 2) as m:
                for k in range(2):
                    for h in range(2):
                        q = 2 * k + h
                        pool.wait_ge(s_staged, m * 4 + (q + 1))
                        pool.nop(nofuse=True)
                        some = pool.value_load(flag[0:1, bass.ds(m * 2 + (k + h * HALF), 1)], min_val=0, max_val=C * P)
                        with pool.If(some > 0):
                            for t in range(C):
                                pool.indirect_dma_start(
                                    out=sorted_list,
                                    out_offset=bass.IndirectOffsetOnAxis(ap=addr_now[:, q, t:t + 1], axis=0),
                                    in_=value_now[:, q, t:t + 1], in_offset=None,
                                    bounds_check=STP * P - 1, oob_is_err=False).then_inc(s_scatter[q], 16)
            all_landed = [pool.value_load(landed[0:1, q % 2, HALF + q // 2:HALF + q // 2 + 1], min_val=16,
                                          max_val=LANDED_MAX) for q in range(4)]
            for q in range(4):
                pool.wait_ge(s_scatter[q], all_landed[q])
            pool.sem_inc(s_sorted, 1)

            n = pool.value_load(bodies[0:1, 0:1], min_val=1, max_val=ST // C)
            pool.wait_ge(s_stored[0], 16 * ((FQ + XQ + 1) // 2))
            pool.wait_ge(s_stored[1], 16 * ((FQ + XQ) // 2))
            pool.wait_ge(s_part_turned, 2 * (FQ + XQ))
            with pool.Fori(0, n) as i:
                for h in range(4):
                    pool.wait_ge(s_receivers, i * 4 + (h + 1))
                    pool.nop(nofuse=True)
                    for k in range(G):
                        pool.indirect_dma_start(
                            out=B_now[:, h, k, :], out_offset=None, in_=B_rows,
                            in_offset=bass.IndirectOffsetOnAxis(ap=dst_now[:, h, k:k + 1], axis=0))\
                            .then_inc(s_gather[h], 16)

            pool.wait_ge(s_sums_done, 1)
            with pool.Fori(0, XQ // 2) as i:
                for k in range(2):
                    pool.wait_ge(s_agg_turned, i * 2 + (k + 1))
                    pool.tensor_copy(agg_now[:, k], agg_flat[:, bass.ds(i * (2 * SD) + k * SD, SD)])\
                        .then_inc(s_agg_now, 1)

        @block.scalar
        def _(act):
            def copy_turned(p, c, w):
                act.wait_ge(s_part_turned, p + 1)
                nc.scalar.copy(turned[:, c, 0:w * P], bank[5][:, 0:w * P]).then_inc(s_part_copied, 1)

            act.wait_ge(s_slab_blank, 1)

            def factor_slab(q, slot):
                for c, (first, w) in enumerate(PARTS):
                    copy_turned(q * 2 + c, c, w)
                    act.wait_ge(s_products, q * 2 + (c + 1))
                    nc.scalar.copy(outs[:, slot, first * D:(first + w) * D], bank[6][:, 0:w * D])\
                        .then_inc(s_rows_out, 1)

            for q in range(2):
                factor_slab(q, q)
            with act.Fori(1, FQ // 2) as i:
                for k in range(2):
                    act.wait_ge(s_stored[k], i * 16)
                    factor_slab(i * 2 + k, k)
            act.wait_ge(s_stored[0], 16 * (FQ // 2))
            factor_slab(FQ - 1, 0)

            act.wait_ge(s_tables, 1)

            def x_part(a, slot, c):
                first, w = PARTS[c]
                p = a * 2 + (2 * FQ + c)
                cols = bass.ds(a * SD + first * D, w * D)
                copy_turned(p, c, w)
                act.wait_ge(s_products, p + 1)
                nc.scalar.copy(A_parts[0][:, cols], bank[6][:, 0:w * D]).then_inc(s_high, 1)
                nc.scalar.copy(outs[:, slot, first * D:(first + w) * D], bank[7][:, 0:w * D]).then_inc(s_rows_out, 1)
                act.wait_ge(s_r1, a * 2 + (c + 2))
                nc.scalar.copy(A_parts[1][:, cols], r1[:, 0:w * D]).then_inc(s_mid, 1)

            def stage_places(i, k, h):
                q = 2 * k + h
                act.wait_ge(s_placed, i * 2 + (h + 1))
                act.wait_ge(s_scatter[q], act.value_load(landed[0:1, h, bass.ds(i, 1)], min_val=16,
                                                         max_val=LANDED_MAX))
                cols = bass.ds(i * C + h * (HALF * C), C)
                nc.scalar.copy(addr_now[:, q, :], place[:, cols])
                nc.scalar.copy(value_now[:, q, :], value[:, cols]).then_inc(s_staged, 1)

            def x_round(i, k, stored):
                slot = (FQ + k) % 2
                act.wait_ge(s_stored[slot], stored)
                for h in range(2):
                    x_part(i, slot, h)
                    if not (isinstance(i, int) and i < 2):
                        act.wait_ge(s_staged, i * 2 + (h - 3))
                    stage_places(i, k, h)

            for k in range(2):
                x_round(k, k, 16 * ((FQ + k) // 2))
            with act.Fori(1, XQ // 2) as m:
                for k in range(2):
                    x_round(m * 2 + k, k, m * 16 + 16 * ((FQ + k) // 2))
            with act.Fori(XQ // 2, HALF // 2) as m:
                for k in range(2):
                    for h in range(2):
                        act.wait_ge(s_staged, m * 4 + (2 * k + h - 3))
                        stage_places(m * 2 + k, k, h)

            act.wait_ge(s_counted, 1)
            with act.Fori(0, XQ) as j:
                first, w = PARTS[1]
                act.wait_ge(s_clamped_sum, j * 2 + 2)
                for t in range(w):
                    ins = nc.scalar.activation(agg_flat[:, bass.ds(j * SD + (first + t) * D, D)],
                                               bank[6][:, t * D:(t + 1) * D], ACT.Relu,
                                               scale=clamped_count[:, bass.ds(j * SLAB + (first + t), 1)])
                ins.then_inc(s_clamped_act, 1)

            act.wait_ge(s_sort_cols, 1)
            for h in range(4):
                nc.scalar.copy(dst_now[:, h, :], dst_s[:, G * h:G * h + G]).then_inc(s_receivers, 1)
            n = act.value_load(bodies[0:1, 0:1], min_val=1, max_val=ST // C)
            act.wait_ge(s_sort_cols, STURNS)

            def copy_one_hots_T(g, slot):
                act.wait_ge(s_oh_turned, g + 1)
                nc.scalar.copy(oh_sT[:, slot], bank[slot][:].bitcast(BF16)[:, 0:G * P]).then_inc(s_oh_copied, 1)

            copy_one_hots_T(0, 0)
            with act.Fori(0, n) as i:
                for h in range(4):
                    copy_one_hots_T(i * 4 + (h + 1), (h + 1) % 2)
                    act.wait_ge(s_summed, i * 4 + (h + 1))
                    nc.scalar.copy(oh32[:, h % 2], oh_s[:, h].rearrange("p n k -> p k n"))
                    act.wait_ge(s_added, i * 4 + (h + 1))
                    nc.scalar.activation(msg[:, h % 2], pre[:, h % 2], ACT.Relu).then_inc(s_msg, 1)
                    act.wait_ge(s_gather[h], i * (16 * G) + 16 * G)
                    nc.scalar.copy(dst_now[:, h, :], dst_s[:, bass.ds(i * C + (C + G * h), G)])\
                        .then_inc(s_receivers, 1)

            def copy_agg_T(a, slot):
                act.wait_ge(s_agg_turned, a + 3)
                for c, (lo, w) in enumerate(halves):
                    ins = nc.scalar.copy(aggT[:, slot, lo:lo + w], bank[2 * slot + c][:, 0:w])
                ins.then_inc(s_aT, 1)

            def finish(a, slot, more):
                if more:
                    copy_agg_T(a + 1, 1 - slot)
                act.wait_ge(s_hidden, a + 1)
                nc.scalar.activation(hid[:, slot], hid[:, slot], ACT.Relu).then_inc(s_relu, 1)
                act.wait_ge(s_var, a + 1)
                nc.scalar.activation(rstd[:, 0, :], mv[:, :, 1], ACT.Sqrt, bias=eps[:, 0:1]).then_inc(s_std, 1)

            act.wait_ge(s_sums_done, 1)
            copy_agg_T(0, 0)
            with act.Fori(0, XQ // 2 - 1) as i:
                for k in range(2):
                    finish(i * 2 + k, k, True)
            finish(XQ - 2, 0, True)
            finish(XQ - 1, 1, False)

        @block.vector
        def _(dve):
            step = [0]

            def link(ins):
                step[0] += 1
                ins.then_inc(s_step, 1)
                dve.wait_ge(s_step, step[0])

            raw_hi = value[:].bitcast(I32)
            raw_lo = place[:].bitcast(I32)
            dve.wait_ge(s_edges, 96 if rest else 64)
            nc.vector.tensor_scalar(raw_hi, edge_raw[:, 0, 0:NT], 7, None, ALU.arith_shift_right)
            link(nc.vector.tensor_scalar(raw_lo, edge_raw[:, 0, 0:NT], 127, None, ALU.bitwise_and))
            nc.vector.tensor_copy(edge_row[:, 0, :], raw_hi)
            nc.vector.tensor_copy(edge_row[:, 1, :], raw_lo)
            nc.vector.tensor_scalar(edge_row[:, 2, :], edge_raw[:, 1, 0:NT], float(LAST), None, ALU.min)\
                .then_inc(s_rows, 1)

            dve.wait_ge(s_rows, 1)
            for g in range(TURNS):
                w = min(BANK, NT - g * BANK)
                cols = slice(g * BANK, g * BANK + w)
                dve.wait_ge(s_turned, g + 1)
                blk, loc, rec = bank[3][:, 0:w], bank[4][:, 0:w], bank[5][:, 0:w]
                nc.vector.tensor_copy(hi_all[:, cols], blk)
                nc.vector.tensor_scalar(value[:, cols], rec, 256.0, None, ALU.mult)
                link(nc.vector.tensor_scalar(place[:, cols], rec, float(LAST), None, ALU.is_ge))
                nc.vector.scalar_tensor_tensor(out=hi_n[:, cols], in0=place[:, cols], scalar=256.0, in1=blk,
                                               op0=ALU.mult, op1=ALU.add)
                nc.vector.scalar_tensor_tensor(out=r1[:, 0:w], in0=place[:, cols], scalar=256.0, in1=loc,
                                               op0=ALU.mult, op1=ALU.add)
                nc.vector.tensor_tensor(value[:, cols], value[:, cols], loc, ALU.add)
                link(nc.vector.tensor_scalar(is_sorted[:, cols], place[:, cols], -1.0, 1.0, ALU.mult, ALU.add))
                nc.vector.tensor_scalar(lo_c[:, cols], r1[:, 0:w], -256.0, None, ALU.add)
                nc.vector.tensor_scalar(place[:, cols], place[:, cols], BIG, None, ALU.mult).then_inc(s_cols, 1)
                dve.wait_ge(s_cols, g + 1)

            dve.wait_ge(s_const, 9)

            def one_hots(to, iota, keys):
                m, t = to.shape[1], to.shape[2]
                return nc.vector.tensor_tensor(to, iota[:, :, 0:t], keys.unsqueeze(1).to_broadcast([P, m, t]),
                                               ALU.is_equal)

            with dve.Fori(0, HALF) as i:
                for h in range(2):
                    dve.wait_ge(s_count_free, i * 2 + (h + 1))
                    one_hots(oh_n[:, h], iota_hi, hi_n[:, bass.ds(i * (2 * C) + h * C, C)]).then_inc(s_count_oh, 1)

            dve.wait_ge(s_count_free, 2 + ROUNDS)
            for g in range(C // G):
                ins = nc.vector.tensor_copy(count[:, :, g * G:(g + 1) * G],
                                            bank[g][:, 0:GW].rearrange("p (b k) -> p b k", k=G))
            link(ins)
            tot, tiles, ends, zero = small[:, 0], small[:, 1], small[:, 2], small[:, 3]
            nc.vector.memset(zero, 0.0)
            link(nc.vector.tensor_reduce(tot, count[:], AX_X, ALU.add))
            link(nc.vector.tensor_scalar(small_i[:, 0], tot, float(P - 1), None, ALU.add))
            link(nc.vector.tensor_scalar(small_i[:, 1], small_i[:, 0], 7, None, ALU.arith_shift_right))
            link(nc.vector.tensor_copy(tiles, small_i[:, 1]))
            link(nc.vector.tensor_tensor_scan(ends, tiles, zero, 0.0, ALU.add, ALU.add))
            link(nc.vector.tensor_tensor(tot, ends, tiles, ALU.subtract))
            link(nc.vector.tensor_scalar(start_at[:, :, 0], tot, float(P), None, ALU.mult))
            for k in range(1, C):
                link(nc.vector.tensor_tensor(start_at[:, :, k], start_at[:, :, k - 1], count[:, :, k - 1], ALU.add))
            nc.vector.memset(small[:, 5], 0.0).then_inc(s_starts, 1)
            link(nc.vector.tensor_scalar(small_i[0:1, 0, 0:1], ends[0:1, NB - 1:NB], float(C - 1), None, ALU.add))
            link(nc.vector.tensor_scalar(small_i[0:1, 0, 1:2], small_i[0:1, 0, 0:1], C.bit_length() - 1, None,
                                         ALU.arith_shift_right))
            nc.vector.tensor_scalar(bodies[:], small_i[0:1, 0, 1:2], 1.0, None, ALU.max)
            dve.wait_ge(s_flags, 1)
            for c in range(TURNS):
                w = min(BANK, NT - c * BANK)
                ins = nc.vector.tensor_reduce(flag_f[0:1, c * BANK // C:(c * BANK + w) // C],
                                              bank[4 + c][0:1, 0:w].rearrange("p (a b) -> p a b", b=C),
                                              AX_X, ALU.add)
            link(ins)
            nc.vector.tensor_copy(flag[:], flag_f[:])
            nc.vector.memset(landed_f[:], 16.0)
            nc.vector.memset(small[0:1, 4, :], 0.0)
            link(nc.vector.tensor_scalar(flag_f[:], flag_f[:], 1.0, float(16 * C), ALU.min, ALU.mult))
            for k in range(2):
                for h in range(2):
                    ins = nc.vector.tensor_tensor_scan(landed_f[:, h, 2 + k:2 + HALF:2],
                                                       flag_f[:, h * HALF + k:(h + 1) * HALF:2],
                                                       small[0:1, 4, 0:HALF // 2], 16.0, ALU.add, ALU.add)
            link(ins)
            nc.vector.tensor_copy(landed[:], landed_f[:]).then_inc(s_tables, 1)
            dve.wait_ge(s_ends, 1)
            link(nc.vector.tensor_copy(tile_end[0:NB, 0:1], bank[4][0:NB, 0:1]))
            nc.vector.memset(block_of[:, 0:G], 0)
            nc.vector.tensor_scalar(block_le[0:NB, :], tile_iota[0:NB, :], tile_end[0:NB, 0:1], None, ALU.is_ge)\
                .then_inc(s_block_le, 1)
            dve.wait_ge(s_blocks, 1)
            for c in range(STURNS):
                w = min(BANK, STP - c * BANK)
                ins = nc.vector.tensor_scalar(block_of[:, G + c * BANK:G + c * BANK + w], bank[4 + c][0:1, 0:w],
                                              float(NB - 1), float(P), ALU.min, ALU.mult)
            ins.then_inc(s_block_of, 1)

            dve.wait_ge(s_b_last, 48)
            link(nc.vector.tensor_copy(b_split[:, 0], b_last[:]))
            link(nc.vector.tensor_tensor(b_left[:, 0], b_last[:], b_split[:, 0], ALU.subtract))
            link(nc.vector.tensor_copy(b_split[:, 1], b_left[:, 0]))
            link(nc.vector.tensor_tensor(b_split[:, 2], b_left[:, 0], b_split[:, 1], ALU.subtract))
            link(nc.vector.tensor_scalar(b_left[:, 1], b_split[:, 0], ident[0:3, 0:1], None, ALU.mult))
            link(nc.vector.scalar_tensor_tensor(out=b_left[:, 0], in0=b_split[:, 1], scalar=ident[0:3, 1:2],
                                                in1=b_left[:, 1], op0=ALU.mult, op1=ALU.add))
            nc.vector.scalar_tensor_tensor(out=b_parts[:], in0=b_split[:, 2], scalar=ident[0:3, 2:3],
                                           in1=b_left[:, 0], op0=ALU.mult, op1=ALU.add).then_inc(s_b_parts, 1)

            def rank_round(i, h, a):
                u = i * 2 + h
                cols = bass.ds(i * C + h * (HALF * C), C)
                dve.wait_ge(s_rank_free, u + 1)
                one_hots(oh_n[:, h], iota_hi, hi_n[:, cols]).then_inc(s_rank_oh, 1)
                dve.wait_ge(s_hist_free, u + 1)
                one_hots(oh_lo, iota_lo, lo_c[:, cols])
                one_hots(oh_hi, iota_hi, hi_all[:, cols]).then_inc(s_hist_oh, 1)
                if a is not None:
                    first, w = PARTS[h]
                    dve.wait_ge(s_high, u + 1)
                    a_cols = bass.ds(a * SD + first * D, w * D)
                    nc.vector.tensor_tensor(r1[:, 0:w * D], bank[6][:, 0:w * D], A_parts[0][:, a_cols],
                                            ALU.subtract).then_inc(s_r1, 1)
                dve.wait_ge(s_before, u + 1)
                for t in range(C):
                    ins = nc.vector.tensor_tensor_reduce(
                        out=count[:, :, t],
                        in0=bank[t // G][:, 0:GW].rearrange("p (b k) -> p b k", k=G)[:, :, t % G],
                        in1=oh_n[:, h, :, t], scale=1.0, scalar=0.0, op0=ALU.mult, op1=ALU.add,
                        accum_out=rank_now[:, t:t + 1])
                ins.then_inc(s_ranked, 1)
                dve.wait_ge(s_ranked, u + 1)
                nc.vector.tensor_tensor(place[:, cols], place[:, cols], rank_now[:], ALU.add).then_inc(s_placed, 1)
                if a is not None:
                    dve.wait_ge(s_mid, u + 1)
                    nc.vector.tensor_tensor(A_parts[2][:, a_cols], r1[:, 0:w * D], A_parts[1][:, a_cols],
                                            ALU.subtract).then_inc(s_low, 1)
                    dve.wait_ge(s_low, u + 1)

            with dve.Fori(0, XQ) as i:
                for h in range(2):
                    rank_round(i, h, i)
            with dve.Fori(XQ, HALF) as i:
                for h in range(2):
                    rank_round(i, h, None)

            dve.wait_ge(s_hist_free, 1 + ROUNDS)
            dve.wait_ge(s_rank_free, 2 + ROUNDS)
            for h in range(4):
                dve.wait_ge(s_scatter[h], 16)
            nc.vector.tensor_copy(clamped_count[:], bank[4][:, 0:NB]).then_inc(s_counted, 1)
            dve.wait_ge(s_counted, 1)
            with dve.Fori(0, XQ) as j:
                first, w = PARTS[0]
                dve.wait_ge(s_clamped_sum, j * 2 + 1)
                for t in range(w):
                    ins = nc.vector.tensor_scalar(agg_flat[:, bass.ds(j * SD + (first + t) * D, D)],
                                                  bank[5][:, t * D:(t + 1) * D], 0.0,
                                                  clamped_count[:, bass.ds(j * SLAB + (first + t), 1)],
                                                  ALU.max, ALU.mult)
                ins.then_inc(s_clamped_dve, 1)

            for c in range(STURNS):
                w = min(BANK, STP - c * BANK)
                cols = slice(c * BANK, c * BANK + w)
                dve.wait_ge(s_sort_turned, c + 1)
                link(nc.vector.tensor_copy(sort_i[:, 0:w], bank[c][:, 0:w]))
                nc.vector.tensor_scalar(dst_s[:, cols], sort_i[:, 0:w], 8, None, ALU.arith_shift_right)
                link(nc.vector.tensor_scalar(sort_l[:, 0:w], sort_i[:, 0:w], 255, None, ALU.bitwise_and))
                nc.vector.tensor_copy(lo_s[:, cols], sort_l[:, 0:w]).then_inc(s_sort_cols, 1)
            nc.vector.memset(oh32[:, 1], 0.0)
            nc.vector.memset(msg[:, 1], 0.0).then_inc(s_msg, 1)

            n = dve.value_load(bodies[0:1, 0:1], min_val=1, max_val=ST // C)
            dve.sem_inc(s_agg, 1)
            dve.wait_ge(s_sort_cols, STURNS)
            dve.wait_ge(s_clamped_dve, XQ + 1)
            dve.wait_ge(s_clamped_act, XQ + 1)
            dve.wait_ge(s_block_of, 1)

            def load_blocks(engine, first, count_):
                return nc.values_load_multi_w_load_instructions(
                    block_of[:, bass.ds(first, count_)], engines=(engine,), min_val=0, max_val=(NB - 1) * P,
                    skip_runtime_bounds_check_because=IN_TABLE)[1]

            one_hots(oh_s[:, 0], iota_lo, lo_s[:, 0:G]).then_inc(s_oh_s, 1)
            with dve.Fori(0, n) as i:
                offsets = load_blocks(mybir.EngineType.DVE, i * C, C)
                for h in range(4):
                    g = i * 4 + h
                    one_hots(oh_s[:, (h + 1) % 4], iota_lo, lo_s[:, bass.ds(i * C + G * (h + 1), G)])\
                        .then_inc(s_oh_s, 1)
                    dve.wait_ge(s_spread, g + 1)
                    dve.wait_ge(s_gather[h], i * (16 * G) + 16 * G)
                    nc.vector.tensor_tensor(pre[:, h % 2], bank[2 + h % 2][:],
                                            B_now[:, h].rearrange("p k n -> p (k n)"), ALU.add).then_inc(s_added, 1)
                    dve.wait_ge(s_summed, g + 2)
                    for k in range(G):
                        cols = bass.ds(offsets[G * h + k], D)
                        dve.wait_ge(s_agg, i * C + (G * h + k + 1))
                        nc.vector.tensor_tensor(agg_flat[:, cols], agg_flat[:, cols],
                                                bank[4 + (h + 1) % 2][:, k * D:(k + 1) * D], ALU.add)\
                            .then_inc(s_agg, 1)
            offsets = load_blocks(mybir.EngineType.DVE, n * C, G)
            dve.wait_ge(s_summed, n * 4 + 2)
            for k in range(G):
                cols = bass.ds(offsets[k], D)
                dve.wait_ge(s_agg, n * C + (k + 1))
                nc.vector.tensor_tensor(agg_flat[:, cols], agg_flat[:, cols], bank[5][:, k * D:(k + 1) * D],
                                        ALU.add).then_inc(s_agg, 1)
            dve.wait_ge(s_agg, n * C + (G + 1))
            nc.vector.memset(small[:, 3], 0.0).then_inc(s_sums_done, 1)

            def finish(a, slot):
                dve.wait_ge(s_h, a + 1)
                for c, (lo, w) in enumerate(halves):
                    ins = nc.vector.tensor_tensor(hid[:, slot, lo:lo + w], bank[4 + 2 * slot + c][:, 0:w],
                                                  H_now[:, slot, lo:lo + w], ALU.add)
                ins.then_inc(s_hidden, 1)
                dve.wait_ge(s_relu, a + 1)
                nc.vector.scalar_tensor_tensor(out=resid[:, slot], in0=slab[:, slot], scalar=2.0, in1=hid[:, slot],
                                               op0=ALU.mult, op1=ALU.add).then_inc(s_resid, 1)
                dve.wait_ge(s_resid, a + 1)
                for t in range(SLAB):
                    ins = nc.vector.bn_stats(stats[:, t, :], resid[:, slot, t * D:(t + 1) * D])
                ins.then_inc(s_stats, 1)
                dve.wait_ge(s_stats, a + 1)
                dve.nop(nofuse=True)
                for t in range(SLAB):
                    ins = nc.vector.bn_aggr(mv[:, t, :], stats[:, t, :])
                ins.then_inc(s_var, 1)
                dve.wait_ge(s_std, a + 1)
                nc.vector.reciprocal(rstd[:, 1, :], rstd[:, 0, :]).then_inc(s_recip, 1)
                dve.wait_ge(s_recip, a + 1)
                for t in range(SLAB):
                    ins = nc.vector.tensor_scalar(outs[:, slot, t * D:(t + 1) * D],
                                                  resid[:, slot, t * D:(t + 1) * D],
                                                  mv[:, t, 0:1], rstd[:, 1, t:t + 1], ALU.subtract, ALU.mult)
                ins.then_inc(s_y, 1)

            for k in range(2):
                dve.wait_ge(s_x[k], 48)
                finish(k, k)
            with dve.Fori(1, XQ // 2) as i:
                for k in range(2):
                    dve.wait_ge(s_x[k], i * 48 + 48)
                    dve.wait_ge(s_out[k], i * 32)
                    finish(i * 2 + k, k)

        @block.tensor
        def _(pe):
            pe.wait_ge(s_const, 9)
            pe.wait_ge(s_rows, 1)
            for g in range(TURNS):
                if g:
                    pe.wait_ge(s_cols, g)
                for k in range(3):
                    for c in range(min(4, CH - 4 * g)):
                        col = (4 * g + c) * P
                        ins = nc.tensor.transpose(bank[3 + k][:, c * P:(c + 1) * P], edge_row[:, k, col:col + P],
                                                  ident[:])
                ins.then_inc(s_turned, 1)
            pe.wait_ge(s_cols, TURNS)

            def zero_bank(b, width):
                return nc.tensor.matmul(bank[b][:, 0:width], zeros_bf[:, 0:P], zeros_bf[:, 0:width], start=True,
                                        stop=False, skip_group_check=True)

            def turn_part(p, slot, c):
                first, w = PARTS[c]
                for t in range(w):
                    ins = nc.tensor.transpose(bank[5][:, t * P:(t + 1) * P],
                                              slab[:, slot, (first + t) * D:(first + t + 1) * D], ident[:])
                ins.then_inc(s_part_turned, 1)

            def multiply_part(to, c, weights, bias):
                for t in range(PARTS[c][1]):
                    cols = slice(t * D, (t + 1) * D)
                    ins = nc.tensor.matmul(bank[to][:, cols], turned[:, c, cols], weights, start=True,
                                           stop=(bias is None))
                    if bias is not None:
                        ins = nc.tensor.matmul(bank[to][:, cols], ones_f[0:1, :], bias, start=False, stop=True)
                return ins

            def count_round(u, h):
                pe.wait_ge(s_count_oh, u + 1)
                for g in range(C // G):
                    ins = nc.tensor.matmul(bank[g][:, 0:GW], ones_bf[:], oh_n[:, h, :, g * G:(g + 1) * G],
                                           start=False, stop=False, skip_group_check=True)
                ins.then_inc(s_count_free, 1)

            def factor_round(q, slot, loads):
                pe.wait_ge(s_slab[slot], loads)
                for c in range(2):
                    p = q * 2 + c
                    turn_part(p, slot, c)
                    count_round(p, c)
                    pe.wait_ge(s_part_copied, p + 1)
                    pe.wait_ge(s_rows_out, p + 1)
                    multiply_part(6, c, wm[:, 1, :], None).then_inc(s_products, 1)

            for g in range(C // G):
                ins = zero_bank(g, GW)
            ins.then_inc(s_zeroed, 1)
            pe.sem_inc(s_count_free, 2)
            pe.sem_inc(s_rows_out, 1)
            pe.sem_inc(s_r1, 1)
            pe.wait_ge(s_weights, 64)
            with pe.Fori(0, FQ // 2) as i:
                for k in range(2):
                    factor_round(i * 2 + k, k, i * 32 + 32)
            factor_round(FQ - 1, 0, 32 * ((FQ + 1) // 2))
            with pe.Fori(FQ, HALF) as i:
                for h in range(2):
                    count_round(i * 2 + h, h)

            pe.wait_ge(s_rows_out, 2 * FQ + 1)
            for c in range(TURNS):
                w = min(BANK, NT - c * BANK)
                ins = nc.tensor.matmul(bank[4 + c][0:1, 0:w], ones_f[:, 0:1], is_sorted[:, c * BANK:c * BANK + w],
                                       start=True, stop=True)
            ins.then_inc(s_flags, 1)
            pe.wait_ge(s_starts, 1)
            for g in range(C // G):
                ins = nc.tensor.matmul(bank[g][:, 0:GW], ident[:], start_at[:, :, g * G:(g + 1) * G],
                                       start=True, stop=False, skip_group_check=True)
            pe.sem_inc(s_rank_free, 2)
            pe.wait_ge(s_tables, 1)
            nc.tensor.transpose(bank[4][0:NB, 0:P], small[:, 2, :], ident[:]).then_inc(s_ends, 1)
            pe.wait_ge(s_block_le, 1)
            for c in range(STURNS):
                w = min(BANK, STP - c * BANK)
                ins = nc.tensor.matmul(bank[4 + c][0:1, 0:w], ones_f[0:NB, 0:1], block_le[0:NB, c * BANK:c * BANK + w],
                                       start=True, stop=True)
            ins.then_inc(s_blocks, 1)
            pe.wait_ge(s_block_of, 1)
            zero_bank(4, NB).then_inc(s_zeroed, 1)
            pe.sem_inc(s_hist_free, 1)

            def rank_round(u, h, slot):
                if slot is not None:
                    turn_part(None, slot, h)
                pe.wait_ge(s_rank_oh, u + 1)
                for g in range(C // G):
                    ins = nc.tensor.matmul(bank[g][:, 0:GW], before[:], oh_n[:, h, :, g * G:(g + 1) * G],
                                           start=False, stop=False, skip_group_check=True)
                ins.then_inc(s_before, 1)
                if slot is not None:
                    pe.wait_ge(s_part_copied, u + (2 * FQ + 1))
                    pe.wait_ge(s_r1, u + 1)
                    pe.wait_ge(s_rows_out, u + (2 * FQ + 1))
                    multiply_part(6, h, wm[:, 0, :], bm_row[:])
                    multiply_part(7, h, wc[:, 0, :], bc_row[:]).then_inc(s_products, 1)
                pe.wait_ge(s_hist_oh, u + 1)
                for t in range(C):
                    ins = nc.tensor.matmul(bank[4][:, 0:NB], oh_lo[:, :, t], oh_hi[:, :, t],
                                           start=False, stop=False, skip_group_check=True)
                ins.then_inc(s_hist_free, 1)
                pe.wait_ge(s_ranked, u + 1)
                for g in range(C // G):
                    ins = nc.tensor.matmul(bank[g][:, 0:GW], from_on[:], oh_n[:, h, :, g * G:(g + 1) * G],
                                           start=False, stop=False, skip_group_check=True)
                ins.then_inc(s_rank_free, 1)

            with pe.Fori(0, XQ // 2) as i:
                for k in range(2):
                    slot = (FQ + k) % 2
                    pe.wait_ge(s_slab[slot], i * 32 + 32 * ((FQ + k) // 2 + 1))
                    for h in range(2):
                        rank_round(i * 4 + (2 * k + h), h, slot)
            with pe.Fori(XQ, HALF) as i:
                for h in range(2):
                    rank_round(i * 2 + h, h, None)

            pe.wait_ge(s_b_parts, 1)
            pe.wait_ge(s_low, 2 * XQ)
            pe.wait_ge(s_rows_out, 2 * (FQ + XQ) + 1)
            pe.sem_inc(s_clamped_dve, 1)
            pe.sem_inc(s_clamped_act, 1)
            with pe.Fori(0, XQ) as j:
                for c, (first, w) in enumerate(PARTS):
                    pe.wait_ge(s_clamped_dve if c == 0 else s_clamped_act, j + 1)
                    for t in range(w):
                        cols = slice(t * D, (t + 1) * D)
                        for part in A_parts:
                            nc.tensor.matmul(bank[5 + c][:, cols], ident_bf[:],
                                             part[:, bass.ds(j * SD + (first + t) * D, D)],
                                             start=(part is A_parts[0]), stop=False)
                        ins = nc.tensor.matmul(bank[5 + c][:, cols], ones_bf[0:3, :], b_parts[:], start=False, stop=True)
                    ins.then_inc(s_clamped_sum, 1)

            for c in range(SCH):
                if c % 4 == 0:
                    pe.wait_ge(s_list_back[c // 4], 16)
                ins = nc.tensor.transpose(bank[c // 4][:, c % 4 * P:(c % 4 + 1) * P],
                                          sorted_rows[:, c * P:(c + 1) * P], ident[:])
                if c % 4 == 3 or c == SCH - 1:
                    ins.then_inc(s_sort_turned, 1)

            n = pe.value_load(bodies[0:1, 0:1], min_val=1, max_val=ST // C)
            pe.wait_ge(s_sort_cols, STURNS)

            def load_blocks(first, count_):
                return nc.values_load_multi_w_load_instructions(
                    block_of[:, bass.ds(first, count_)], engines=(mybir.EngineType.PE,), min_val=0,
                    max_val=(NB - 1) * P, skip_runtime_bounds_check_because=IN_TABLE)[1]

            def turn_one_hots(g, buf, slot):
                pe.wait_ge(s_oh_s, g + 1)
                for k in range(G):
                    ins = nc.tensor.transpose(bank[slot][:].bitcast(BF16)[:, k * P:(k + 1) * P], oh_s[:, buf, :, k],
                                              ident_bf[:])
                ins.then_inc(s_oh_turned, 1)

            def spread(g, slot, offsets):
                pe.wait_ge(s_oh_copied, g + 1)
                for k in range(G):
                    for part in A_parts:
                        ins = nc.tensor.matmul(bank[2 + slot][:, k * D:(k + 1) * D], oh_sT[:, slot, k * P:(k + 1) * P],
                                               part[:, bass.ds(offsets[k], D)], start=(part is A_parts[0]),
                                               stop=(part is A_parts[2]))
                ins.then_inc(s_spread, 1)

            turn_one_hots(0, 0, 0)
            spread(0, 0, load_blocks(G, G))
            pe.sem_inc(s_summed, 1)
            with pe.Fori(0, n) as i:
                offsets = load_blocks(i * C + 2 * G, C)
                for h in range(4):
                    turn_one_hots(i * 4 + (h + 1), (h + 1) % 4, (h + 1) % 2)
                    pe.wait_ge(s_msg, i * 4 + (h + 1))
                    for k in range(G):
                        ins = nc.tensor.matmul(bank[4 + (h + 1) % 2][:, k * D:(k + 1) * D], oh32[:, (h + 1) % 2, k, :],
                                               msg[:, (h + 1) % 2, k * D:(k + 1) * D], start=True, stop=True)
                    ins.then_inc(s_summed, 1)
                    spread(i * 4 + (h + 1), (h + 1) % 2, offsets[G * h:G * h + G])
            pe.wait_ge(s_msg, n * 4 + 1)
            for k in range(G):
                ins = nc.tensor.matmul(bank[5][:, k * D:(k + 1) * D], oh32[:, 1, k, :],
                                       msg[:, 1, k * D:(k + 1) * D], start=True, stop=True)
            ins.then_inc(s_summed, 1)

            def turn_agg(a, slot):
                pe.wait_ge(s_agg_now, a + 1)
                for t in range(SLAB):
                    ins = nc.tensor.transpose(bank[2 * slot + t // 4][:, t % 4 * P:(t % 4 + 1) * P],
                                              agg_now[:, slot, t * D:(t + 1) * D], ident[:])
                ins.then_inc(s_agg_turned, 1)

            def multiply_agg(a, slot):
                pe.wait_ge(s_aT, a + 1)
                for t in range(SLAB):
                    ins = nc.tensor.matmul(bank[4 + 2 * slot + t // 4][:, t % 4 * D:(t % 4 + 1) * D],
                                           aggT[:, slot, t * P:(t + 1) * P], wc[:, 1, :], start=True, stop=True)
                ins.then_inc(s_h, 1)

            pe.wait_ge(s_sums_done, 1)
            pe.sem_inc(s_agg_turned, 2)
            turn_agg(0, 0)
            turn_agg(1, 1)
            for k in range(2):
                multiply_agg(k, k)
                turn_agg(k + 2, k)
            with pe.Fori(1, XQ // 2 - 1) as i:
                for k in range(2):
                    pe.wait_ge(s_hidden, i * 2 + (k - 1))
                    multiply_agg(i * 2 + k, k)
                    turn_agg(i * 2 + (k + 2), k)
            for k in range(2):
                pe.wait_ge(s_hidden, XQ - 3 + k)
                multiply_agg(XQ - 2 + k, k)


_INS = ["x", "src", "dst", "L0_gnn_factors", "L0_gnn_Wm", "L0_gnn_bm", "L0_gnn_Wc", "L0_gnn_bc"]


def kernel(**inputs):
    import numpy as _np
    import concourse.bacc as _bacc
    from concourse import mybir as _mybir
    from concourse.bass_utils import run_bass_kernel_spmd as _run

    nc = _bacc.Bacc("TRN2", target_bir_lowering=False, num_devices=1)
    arrays, args = {}, []
    for name in _INS:
        a = _np.ascontiguousarray(inputs[name])
        arrays[f"in_{name}_dram"] = a
        args.append(nc.dram_tensor(f"in_{name}_dram", a.shape, _mybir.dt.from_np(a.dtype), kind="ExternalInput").ap())
    shape = inputs["x"].shape
    args.append(nc.dram_tensor("out_dram", shape, _mybir.dt.float32, kind="ExternalOutput").ap())
    gnn_kernel(nc, *args)
    r = _run(nc, [arrays], core_ids=[0])
    return r.results[0]["out_dram"]
```
